# Optimizing a Trainium2 kernel written in Bass

```python
import numpy as np
import jax
import jax.numpy as jnp

def _softmax(x, axis=-1):
    return jax.nn.softmax(x, axis=axis)
def _gelu(x):
    return jax.nn.gelu(x, approximate=True)
def _silu(x):
    return jax.nn.silu(x)
def _sigmoid(x):
    return jax.nn.sigmoid(x)
def _layernorm(x, axis=-1, eps=1e-5):
    m = jnp.mean(x, axis=axis, keepdims=True)
    v = jnp.var(x, axis=axis, keepdims=True)
    return (x - m) / jnp.sqrt(v + eps)
def _scatter_add(tgt, idx, src, axis=0):
    return tgt.at[idx].add(src)
def _segment_sum(src, seg, n):
    return jax.ops.segment_sum(src, seg, n)

kernel_name = 'mk_conv_preact_d2_conv_nhwc256_80073b'

def setup_inputs(seed: int = 0):
    np.random.seed(seed)
    _w = jnp.asarray
    def _rec_inputs():
        import jax
        import jax.numpy as jnp
        _gk = jax.random.key(seed)
        x = -0.000125 + 0.9999 * jax.random.normal(jax.random.fold_in(_gk, 1), (8, 128, 128, 256), jnp.float32)
        return x
    x = _rec_inputs()
    def _L0_conv_setup():
        import jax, jax.numpy as jnp
        import numpy as np
        B, H, W, C = (8, 128, 128, 256)
        key = jax.random.key(seed)
        k1, k2 = jax.random.split(key)
        x = jax.random.normal(k1, (B, H, W, C), dtype=jnp.float32)
        gamma = jax.random.normal(k2, (), dtype=jnp.float32)
        return {'x': x, 'gamma': gamma}
    _L0_conv_all = _L0_conv_setup()
    _L0_conv_in = {k: v for k, v in _L0_conv_all.items() if k in ('gamma', )}
    del _L0_conv_all

    def _L1_conv_setup():
        import jax, jax.numpy as jnp
        import numpy as np
        B, H, W, C = (32, 64, 64, 256)
        CROP = 48
        ITER_N = 5

        def _conv2d_same(y, w, b):
            out = jax.lax.conv_general_dilated(y, w, window_strides=(1, 1), padding='SAME', dimension_numbers=('NHWC', 'HWIO', 'NHWC'))
            return out + b
        key = jax.random.key(seed)
        k0, k1, k2 = jax.random.split(key, 3)
        x = jax.random.normal(k0, (B, H, W, C), dtype=jnp.float32)
        w1 = jax.random.normal(k1, (3, 3, C, C), dtype=jnp.float32) * 0.02
        b1 = jnp.zeros((C,), dtype=jnp.float32)
        w2 = jax.random.normal(k2, (3, 3, C, C), dtype=jnp.float32) * 0.02
        b2 = jnp.zeros((C,), dtype=jnp.float32)
        return {'x': x, 'w1': w1, 'b1': b1, 'w2': w2, 'b2': b2}
    _L1_conv_all = _L1_conv_setup()
    _L1_conv_in = {k: v for k, v in _L1_conv_all.items() if k in ('w1', 'b1', 'w2', 'b2', )}
    del _L1_conv_all

    return {
        "x": x,
        "L0_conv_gamma": _L0_conv_in["gamma"],
        "L1_conv_w1": _L1_conv_in["w1"],
        "L1_conv_b1": _L1_conv_in["b1"],
        "L1_conv_w2": _L1_conv_in["w2"],
        "L1_conv_b2": _L1_conv_in["b2"],
    }

def reference(x, L0_conv_gamma, L1_conv_w1, L1_conv_b1, L1_conv_w2, L1_conv_b2):
    import jax
    import jax.numpy as jnp
    def _L0_conv_ref(x, gamma):
        import jax, jax.numpy as jnp
        import numpy as np
        B, H, W, C = (8, 128, 128, 256)
        xp = jnp.transpose(x, (0, 3, 2, 1))
        b, c, w, h = xp.shape
        p = xp.reshape(b, c, w * h)
        q = jnp.swapaxes(p, 1, 2)
        s = jnp.einsum('bcn,bnd->bcd', p, q)
        m = jax.nn.softmax(s, axis=-1)
        n = jnp.einsum('bnc,bcd->bnd', q, m)
        n_new = jnp.swapaxes(n, 1, 2).reshape(b, c, w, h)
        out = gamma * n_new + xp
        return jnp.transpose(out, (0, 3, 2, 1))

    def _L1_conv_ref(x, w1, b1, w2, b2):
        import jax, jax.numpy as jnp
        import numpy as np
        B, H, W, C = (32, 64, 64, 256)
        CROP = 48
        ITER_N = 5

        def _conv2d_same(y, w, b):
            out = jax.lax.conv_general_dilated(y, w, window_strides=(1, 1), padding='SAME', dimension_numbers=('NHWC', 'HWIO', 'NHWC'))
            return out + b
        b, h, w_, c = x.shape
        ch, cw = (min(CROP, h), min(CROP, w_))
        oh, ow = ((h - ch) // 2, (w_ - cw) // 2)
        x_sub = x[:, oh:oh + ch, ow:ow + cw, :]
        M = ch * cw
        xs = x_sub.reshape(b, c, M)
        Minv = jnp.float32(1.0 / M)
        I_hat = Minv * (jnp.eye(M, dtype=x.dtype) - Minv * jnp.ones((M, M), dtype=x.dtype))
        cov = jnp.einsum('bcm,mn,bdn->bcd', xs, I_hat, xs)
        I3 = 3.0 * jnp.eye(c, dtype=x.dtype)
        normA = jnp.einsum('bii->b', cov)
        A = cov / normA[:, None, None]
        ZY = 0.5 * (I3 - A)
        Y = jnp.matmul(A, ZY)
        Z = ZY
        for _ in range(1, ITER_N - 1):
            ZY = 0.5 * (I3 - jnp.matmul(Z, Y))
            Y = jnp.matmul(Y, ZY)
            Z = jnp.matmul(ZY, Z)
        ZY = 0.5 * jnp.matmul(Y, I3 - jnp.matmul(Z, Y))
        y = ZY * jnp.sqrt(normA)[:, None, None]
        y = jnp.mean(y, axis=-1).reshape(b, 1, 1, c)
        y = jax.nn.relu(_conv2d_same(y, w1, b1))
        y = jax.nn.sigmoid(_conv2d_same(y, w2, b2))
        return y * x

    def _gn(v, G=32, eps=1e-5):
        B_, H_, W_, C_ = v.shape
        g = v.reshape(B_, H_, W_, G, C_ // G)
        m = jnp.mean(g, axis=(1, 2, 4), keepdims=True)
        s = jnp.var(g, axis=(1, 2, 4), keepdims=True)
        return ((g - m) / jnp.sqrt(s + eps)).reshape(v.shape)

    def _ln_c(v, eps=1e-6):
        m = jnp.mean(v, axis=-1, keepdims=True)
        s = jnp.var(v, axis=-1, keepdims=True)
        return (v - m) / jnp.sqrt(s + eps)

    def _ln_t(v, eps=1e-5):
        m = jnp.mean(v, axis=-1, keepdims=True)
        s = jnp.var(v, axis=-1, keepdims=True)
        return (v - m) / jnp.sqrt(s + eps)

    def _to_tokens(v):
        B_, H_, W_, C_ = v.shape
        return v.reshape(B_, H_ * W_, C_)
    def _from_tokens(t, like):
        return t.reshape(like.shape)

    x = x + _L0_conv_ref(_gn(x), L0_conv_gamma)
    x = x + _L1_conv_ref(_gn(x), L1_conv_w1, L1_conv_b1, L1_conv_w2, L1_conv_b2)
    return x


_drawn_inputs = setup_inputs


def setup_inputs(seed=0):
    import zlib

    import numpy as np

    out = dict(_drawn_inputs(seed))
    spreads = {'L1_conv_b1': (0.0, 0.8), 'L1_conv_b2': (0.0, 0.3)}
    factors = {'L1_conv_w1': 200.0, 'L1_conv_w2': 8.0}
    for name, (base, spread) in spreads.items():
        noise = np.random.default_rng([zlib.crc32(name.encode()), seed]).standard_normal(out[name].shape)
        drawn = base * np.exp(spread * noise) if base else spread * noise
        out[name] = jnp.asarray(drawn.astype(out[name].dtype))
    for name, factor in factors.items():
        out[name] = (out[name] * factor).astype(out[name].dtype)
    return out
```

```python
import concourse.bass as bass
from concourse import mybir
from contextlib import ExitStack

f32 = mybir.dt.float32
f16 = mybir.dt.float16
ALU = mybir.AluOpType
ACT = mybir.ActivationFunctionType
AX = mybir.AxisListType

B, H, W_, C = 8, 128, 128, 256
N = H * W_
P = 128
KB = C // P
GN = C // 32
CROP = 48
CR0 = (H - CROP) // 2
M = CROP * CROP
NJ = M // C
NS_ITER = 5
EPS = 1e-5

CT = 8
CHUNKS = N // (P * CT)
AG = 4
XA = 4
CYC_A = CHUNKS // XA
GPC = XA * CT // AG
HL = 4
POOL_SUMS = (0, 1, 3, 4, 6)
DVE_SUMS = tuple(q for q in range(GPC) if q not in POOL_SUMS)

XC = 4
CG = CT // 2
GRAN = CHUNKS * CG
GCYC = XC * CG
TB = 2
HT = 4
OB = 2
AHEAD = 2

CW = 2 * CROP
CTILES = M // CW
UPX = 3 * CW
UNITS = M // UPX
UROWS = UPX // NJ
CROPMM = [(jj, m) for jj in range((NJ + 1) // 2) for m in range(KB)]

STAGES = ([("crop", 1)] * UNITS
          + [("gram", 1), ("assemble", 1), ("mirror", 1), ("stats", 1), ("rows", 2), ("scores", 2), ("weights", 2),
             ("project", 2), ("squares", 1), ("stats1", 2)]
          + [("crop_product", 1)] * len(CROPMM)
          + [("cov", 1), ("cov_assemble", 1), ("cov_mirror", 1), ("cov_rows", 1), ("trace", 1), ("normal", 1), ("first", 1)]
          + [("zy", 1), ("tyz", 1)] * (NS_ITER - 2)
          + [("zv", 1), ("yu", 1), ("w1", 1), ("w2", 1), ("gate", 1), ("final", 0)])
SPREAD = sum(n for _, n in STAGES)
assert SPREAD <= GRAN
DVE_LINKS = 50


def build(nc, x, gamma, w1, b1, w2, b2, out):
    x_chunks = x.rearrange("b h w c -> (b h w) c").rearrange("(n p t) c -> n p (t c)", p=P, t=CT)
    out_chunks = out.rearrange("b h w c -> (b h w) c").rearrange("(n p t) c -> n p (t c)", p=P, t=CT)
    x_crop = x[:, CR0:CR0 + CROP, CR0:CR0 + CROP, :].rearrange("b (t r) w c -> b r w t c", r=2)
    tap = [w[1, 1, :, :].rearrange("(k p) n -> p k n", p=P) for w in (w1, w2)]

    ctx = ExitStack()
    with ctx:
        def sb(name, shape, dt=f32):
            return ctx.enter_context(nc.sbuf_tensor(name, shape, dt))

        def sem(name):
            return ctx.enter_context(nc.semaphore(name))

        xa = sb("xa", [P, XA, CT * C])
        hl = sb("hl", [P, HL, AG, 2 * C], f16)
        accp = sb("accp", [P, AG * C])
        accd = sb("accd", [P, AG * C])
        xc = sb("xc", [P, XC, CT * C])
        hT = sb("hT", [P, HT, 2, 2, P], f16)
        lT = sb("lT", [P, HT, 2, 2, P], f16)
        ob = sb("ob", [P, OB, CT * C])
        wf = sb("wf", [P, KB, 2, C], f16)
        beta = sb("beta", [P, C])
        xcr = sb("xcr", [CW, CTILES, C])
        xcT = sb("xcT", [P, KB, 2, M], f16)
        ghl = sb("ghl", [P, KB, NJ, 2, C], f16)
        g32 = sb("g32", [P, 2, 2 * C])
        e1 = sb("e1", [P, 3 * P])
        S = sb("S", [P, KB, C])
        Cm = sb("Cm", [P, KB, C])
        V = sb("V", [P, KB, C])
        Wm = sb("Wm", [P, KB, C])
        wsp = sb("wsp", [P, KB, 2, C], f16)
        prod = sb("prod", [P, KB, C])
        e0 = prod[:, :, :].rearrange("p k c -> p (k c)")
        YZ = sb("YZ", [P, KB, 2, C])
        Tm = V
        dg = g32[:, :, :].rearrange("p a (n c) -> p (a n) c", c=P)[:, 0:3 * KB, :].rearrange("p (n k) c -> p n k c", k=KB)
        ident = sb("ident", [P, P])
        i15 = sb("i15", [P, KB, C])
        onesf = sb("onesf", [P, P])
        ones16 = sb("ones16", [P, P], f16)
        zero16 = sb("zero16", [P, 2 * C], f16)
        grp = sb("grp", [P, P])
        nhalf = sb("nhalf", [P, KB])
        half = sb("half", [P, 1])
        w1c = sb("w1c", [P, KB, C])
        w2c = sb("w2c", [P, KB, C])
        b1c = sb("b1c", [P, KB])
        b2c = sb("b2c", [P, KB])
        gam0 = sb("gam0", [1, 1])
        gam = sb("gam", [P, 1])
        st = sb("st", [P, 4])
        gst = sb("gst", [P, 4])
        cc = sb("cc", [P, 3, KB])
        ncc = sb("ncc", [P, 2, KB])
        rhs2 = sb("rhs2", [P, KB, 2])
        ve = sb("ve", [P, KB])
        tmp = sb("tmp", [P, KB])
        nmx = sb("nmx", [P, KB])
        den = sb("den", [P, KB])
        acol = sb("acol", [P, KB])
        bcol = sb("bcol", [P, KB])
        swc = sb("swc", [P, KB])
        st1 = sb("st1", [P, 4])
        gst1 = sb("gst1", [P, 4])
        r1 = sb("r1", [P, KB])
        nb1 = sb("nb1", [P, KB])
        sc = sb("sc", [P, KB])
        nsc = sb("nsc", [P, KB])
        td = sb("td", [P, KB])
        tr = sb("tr", [P, 1])
        itr = sb("itr", [P, 1])
        sq = sb("sq", [P, 1])
        v1 = sb("v1", [P, KB])
        u1 = sb("u1", [P, KB])
        y0 = sb("y0", [P, KB])
        y1 = sb("y1", [P, KB])
        z2 = sb("z2", [P, KB])
        ez = sb("ez", [P, KB])
        y2 = sb("y2", [P, KB])
        ab = sb("ab", [P, 2, KB])

        def bank(name):
            return ctx.enter_context(nc.psum_tensor(name, [P, 512], f32))
        P0, P1, MA, MB = bank("P0"), bank("P1"), bank("MA"), bank("MB")
        TP = [bank(f"TP{i}") for i in range(TB)]
        OP = [bank(f"OP{i}") for i in range(TB)]

        const_in = sem("const_in")
        const_ok = sem("const_ok")
        pool_const = sem("pool_const")
        gam_in, gam_ps, gam_ok = sem("gam_in"), sem("gam_ps"), sem("gam_ok")
        xa_in = [sem(f"xa_in{i}") for i in range(XA)]
        xa_free_dve, xa_free_pool = sem("xa_free_dve"), sem("xa_free_pool")
        h_done, l_done, hl_free = sem("h_done"), sem("l_done"), sem("hl_free")
        accp_done, accd_done = sem("accp_done"), sem("accd_done")
        xc_in = [sem(f"xc_in{i}") for i in range(XC)]
        t_done, hT_done, lT_done = sem("t_done"), sem("hT_done"), sem("lT_done")
        o_done, ob_done = sem("o_done"), sem("ob_done")
        stored = [sem(f"stored{i}") for i in range(OB)]
        crop_in, crop_t, crop_h, crop_l = sem("crop_in"), sem("crop_t"), sem("crop_h"), sem("crop_l")
        cm_done, g_done, ghl_done = sem("cm_done"), sem("g_done"), sem("ghl_done")
        dve_link = sem("dve_link")
        tyz_done, yz_act, yz_dve = sem("tyz_done"), sem("yz_act"), sem("yz_dve")
        zy_done, t_ready = sem("zy_done"), sem("t_ready")
        e = {n: sem("e_" + n) for n in (
            "gram e0 e1 tdone s01 mirror acc sbc st gst ve r dg rows means expo den wsp_h wsp wdone proj prod "
            "squares st1 gst1 ve1 r1 nb1 cov e0c e1c tdonec s01c mirrorc td sc trps tr sq z0 y0ps y0 "
            "v1 zvps u1 yups y0c w1ps y1 w2ps z2 ez ab dg2 rows2 wfh wf crop_free").split()}
        block = ctx.enter_context(nc.Block())

        @block.sync
        def _(sp):
            for dst, src in ((w1c, tap[0]), (w2c, tap[1])):
                sp.dma_start(dst[:, :, :], src).then_inc(const_in, 16)
            for dst, src in ((b1c, b1), (b2c, b2)):
                sp.dma_start(dst[:, :], src.rearrange("(k p) -> p k", p=P),
                             allow_slow_non_contiguous=True).then_inc(const_in, 16)
            sp.dma_start(gam0[:, :], gamma.rearrange("(a n) -> a n", a=1)).then_inc(gam_in, 16)

            def load_a(b):
                with sp.Fori(0, CYC_A) as i:
                    n = sp.snap(i + b * CYC_A)
                    for s in range(XA):
                        sp.wait_ge(xa_free_dve, n * XA + (s + 1))
                        sp.wait_ge(xa_free_pool, n * XA + (s + 1))
                        sp.dma_start(xa[:, s, :], x_chunks[n * XA + s]).then_inc(xa_in[s], 16)

            def load_crop(b):
                for r in range(2):
                    sp.dma_start(xcr[r * CROP:(r + 1) * CROP, :, :], x_crop[b, r]).then_inc(crop_in, 16)

            def load_c(b, t64, c):
                sp.wait_ge(t_done, t64 + (c + 1) * CG)
                sp.dma_start(xc[:, c % XC, :], x_chunks[b * CHUNKS + c]).then_inc(xc_in[c % XC], 16)

            def pass_c(b):
                t64 = sp.snap(b * GRAN)
                bc = sp.snap(b * CHUNKS)
                for c in range(XC):
                    load_c(b, t64, c)
                for c in range(CHUNKS):
                    if c + XC < CHUNKS:
                        load_c(b, t64, c + XC)
                    sp.wait_ge(ob_done, t64 + ((c + 1) * CG + TB))
                    sp.dma_start(out_chunks[bc + c], ob[:, c % OB, :]).then_inc(stored[c % OB], 16)

            load_crop(0)
            load_a(0)
            with sp.Fori(1, B) as b:
                sp.wait_ge(e["crop_free"], b)
                load_crop(b)
                load_a(b)
                pass_c(b - 1)
            pass_c(B - 1)
            for s in range(OB):
                sp.wait_ge(stored[s], 16 * (B * CHUNKS // OB + 1))

        @block.gpsimd
        def _(pool):
            nc.gpsimd.memset(ident[:, :], 0.0)
            nc.gpsimd.memset(grp[:, :], 1.0 / GN)
            nc.gpsimd.memset(onesf[:, :], 1.0)
            nc.gpsimd.memset(ones16[:, :], 1.0)
            nc.gpsimd.memset(nhalf[:, :], -0.5)
            nc.gpsimd.memset(half[:, :], 0.5)
            nc.gpsimd.memset(zero16[:, :], 0.0).then_inc(pool_const, 1)
            pool.wait_ge(pool_const, 1)
            nc.gpsimd.affine_select(out=ident[:, :], in_=ident[:, :], compare_op=ALU.not_equal, fill=1.0,
                                    base=0, pattern=[[-1, P]], channel_multiplier=1).then_inc(pool_const, 1)
            blocks = grp[:, :].rearrange("p (g d) -> p g d", d=GN)
            nc.gpsimd.affine_select(out=blocks, in_=blocks, compare_op=ALU.is_ge, fill=0.0, base=0,
                                    pattern=[[-GN, P // GN], [0, GN]], channel_multiplier=1).then_inc(pool_const, 1)
            pool.wait_ge(pool_const, 3)
            nc.gpsimd.affine_select(out=blocks, in_=blocks, compare_op=ALU.is_ge, fill=0.0, base=GN - 1,
                                    pattern=[[GN, P // GN], [0, GN]], channel_multiplier=-1).then_inc(pool_const, 1)
            pool.sem_inc(xa_free_pool, XA)

            def pass_a(b):
                adds = pool.snap(b * (CYC_A * len(POOL_SUMS) + 1))
                with pool.Fori(0, CYC_A) as i:
                    n = pool.snap(i + b * CYC_A)
                    done = pool.snap(adds + i * len(POOL_SUMS))
                    land = pool.snap(n * 16 + 16)
                    for k, q in enumerate(POOL_SUMS):
                        s = q // 2
                        pool.wait_ge(xa_in[s], land)
                        pool.wait_ge(accp_done, done + (k + 1))
                        grp_x = xa[:, s, (q % 2) * AG * C:(q % 2 + 1) * AG * C]
                        nc.gpsimd.tensor_tensor(accp[:, :], accp[:, :], grp_x, ALU.add).then_inc(accp_done, 1)
                        if k + 1 == len(POOL_SUMS) or POOL_SUMS[k + 1] // 2 != s:
                            pool.wait_ge(accp_done, done + (k + 2))
                            pool.sem_inc(xa_free_pool, 1)

            def middle(n1):
                pool.wait_ge(e["ve"], n1)
                nc.gpsimd.tensor_tensor(cc[:, 0, :], ve[:, :], nhalf[:, :], ALU.pow).then_inc(e["r"], 1)
                pool.wait_ge(e["ve1"], n1)
                nc.gpsimd.tensor_tensor(r1[:, :], ve[:, :], nhalf[:, :], ALU.pow).then_inc(e["r1"], 1)
                pool.wait_ge(e["tr"], n1)
                nc.gpsimd.tensor_tensor(sq[:, :], tr[:, :], half[:, :], ALU.pow).then_inc(e["sq"], 1)

            pass_a(0)
            middle(1)
            with pool.Fori(1, B) as b:
                pass_a(b)
                middle(pool.snap(b + 1))

        @block.scalar
        def _(act):
            act.sem_inc(g_done, 2)

            def pass_a(b):
                with act.Fori(0, CYC_A) as i:
                    n = act.snap(i + b * CYC_A)
                    land = act.snap(n * 16 + 16)
                    g8 = act.snap(n * GPC)
                    for q in range(GPC):
                        s = q // 2
                        act.wait_ge(xa_in[s], land)
                        act.wait_ge(hl_free, g8 + (q + 1))
                        src = xa[:, s, (q % 2) * AG * C:(q % 2 + 1) * AG * C].rearrange("p (t c) -> p t c", t=AG)
                        nc.scalar.activation(hl[:, q % HL, :, 0:C], src, ACT.Copy).then_inc(h_done, 1)

            def split_t(g0, g):
                act.wait_ge(t_done, g0 + (g + 1 + GCYC))
                act.wait_ge(o_done, g0 + (g + 1))
                nc.scalar.activation(hT[:, g % HT].rearrange("p k t c -> p (k t c)"), TP[g % TB][:, :],
                                     ACT.Copy).then_inc(hT_done, 1)

            def pass_c(b):
                with act.Fori(0, GRAN // GCYC) as i:
                    g0 = act.snap(b * GRAN + i * GCYC)
                    for g in range(GCYC):
                        split_t(g0, g)

            def middle(b, n1, filler):
                b16 = act.snap(b * 2 * UNITS)
                bcm = act.snap(b * len(CROPMM))
                bns = act.snap(b * (NS_ITER - 2))
                for u in range(UNITS):
                    for k in range(KB):
                        act.wait_ge(crop_t, b16 + (2 * u + k + 1))
                        nc.scalar.activation(
                            xcT[:, k, 0, :].rearrange("p (j c) -> p j c", j=NJ)[:, :, u * UROWS:(u + 1) * UROWS],
                            (MA, MB)[k][:, 0:UPX].rearrange("p (c j) -> p j c", j=NJ), ACT.Copy).then_inc(crop_h, 1)
                    filler("crop")
                act.wait_ge(e["gram"], n1)
                nc.scalar.activation(e0[:, :], P0[:, :], ACT.Copy).then_inc(e["e0"], 1)
                filler("gram")
                filler("assemble")
                act.wait_ge(e["mirror"], n1)
                nc.scalar.activation(S[:, 1, 0:P], MB[:, 384:512], ACT.Copy).then_inc(e["s01"], 1)
                filler("mirror")
                filler("stats")
                filler("rows")
                act.wait_ge(e["expo"], n1)
                for k in range(KB):
                    last = nc.scalar.activation(V[:, k, :], Cm[:, k, :], ACT.Exp, bias=nmx[:, k:k + 1],
                                                accum_out=den[:, k:k + 1])
                last.then_inc(e["den"], 1)
                filler("scores")
                act.wait_ge(e["wdone"], n1)
                nc.scalar.activation(wsp[:, :, 0, :], Wm[:, :, :], ACT.Copy).then_inc(e["wsp_h"], 1)
                filler("weights")
                filler("project")
                filler("squares")
                act.wait_ge(e["nb1"], n1)
                filler("stats1")
                for i, (jj, m) in enumerate(CROPMM):
                    n = min(2, NJ - 2 * jj) * C
                    act.wait_ge(cm_done, bcm + (i + 1))
                    act.wait_ge(ghl_done, bcm + (i + 1))
                    nc.scalar.activation(g32[:, i % 2, 0:n], (MA, MB)[m][:, 0:n], ACT.Identity,
                                         bias=nb1[:, m:m + 1], scale=r1[:, m:m + 1]).then_inc(g_done, 1)
                    filler("crop_product")
                act.wait_ge(e["cov"], n1)
                nc.scalar.activation(e0[:, :], P0[:, :], ACT.Copy).then_inc(e["e0c"], 1)
                filler("cov")
                filler("cov_assemble")
                act.wait_ge(e["mirrorc"], n1)
                nc.scalar.activation(S[:, 1, 0:P], MB[:, 384:512], ACT.Copy).then_inc(e["s01c"], 1)
                filler("cov_mirror")
                filler("cov_rows")
                filler("trace")
                filler("normal")
                act.wait_ge(e["y0ps"], n1)
                nc.scalar.activation(YZ[:, :, 0, :], MA[:, :].rearrange("p (k c) -> p k c", k=KB),
                                     ACT.Copy).then_inc(e["y0"], 1)
                filler("first")
                for i in range(NS_ITER - 2):
                    filler("zy")
                    act.wait_ge(tyz_done, bns + (i + 1))
                    nc.scalar.activation(YZ[:, 0].rearrange("p a c -> p (a c)"), MA[:, :], ACT.Copy).then_inc(yz_act, 1)
                    filler("tyz")
                filler("zv")
                filler("yu")
                filler("w1")
                act.wait_ge(e["z2"], n1)
                nc.scalar.activation(ez[:, :], z2[:, :], ACT.Exp, scale=-1.0).then_inc(e["ez"], 1)
                filler("w2")
                filler("gate")
                act.wait_ge(e["wfh"], n1)
                act.wait_ge(o_done, b * GRAN + HT)
                nc.scalar.activation(wf[:, :, 0, :], prod[:, :, :], ACT.Copy).then_inc(e["wf"], 1)

            def interleaved(b):
                g0 = act.snap(b * GRAN)
                for g in range(AHEAD):
                    split_t(g0, g)
                at = [0]

                def filler(stage, n=None):
                    for _ in range(dict(STAGES)[stage] if n is None else n):
                        if at[0] + AHEAD < GRAN:
                            split_t(g0, at[0] + AHEAD)
                        at[0] += 1
                return filler

            pass_a(0)
            middle(0, 1, lambda *_: None)
            with act.Fori(1, B) as b:
                n1 = act.snap(b + 1)
                pass_a(b)
                filler = interleaved(act.snap(b - 1))
                filler("", GRAN - SPREAD)
                middle(b, n1, filler)
            pass_c(B - 1)

        @block.vector
        def _(dve):
            dve.wait_ge(pool_const, 4)
            nc.vector.memset(i15[:, :, :], 0.0).then_inc(const_ok, 1)
            dve.wait_ge(const_ok, 1)
            for k in range(KB):
                last = nc.vector.tensor_scalar(i15[:, k, k * P:(k + 1) * P], ident[:, :], 1.5, None, ALU.mult)
            last.then_inc(const_ok, 1)
            dve.wait_ge(const_ok, 2)
            dve.sem_inc(xa_free_dve, XA)
            dve.sem_inc(lT_done, TB)
            dve.sem_inc(ob_done, TB)
            dve.sem_inc(ghl_done, 2)
            dve.sem_inc(crop_l, 2)
            for s in range(OB):
                dve.sem_inc(stored[s], 16)
            dve.wait_ge(gam_ps, 1)
            nc.vector.tensor_copy(gam[:, :], MA[:, 0:1]).then_inc(gam_ok, 1)
            dve.wait_ge(gam_ok, 1)
            dve.wait_ge(const_in, 4 * 16)

            def pass_a(b):
                adds = dve.snap(b * (CYC_A * len(DVE_SUMS) + 1))
                nc.vector.memset(accp[:, :], 0.0).then_inc(accp_done, 1)
                nc.vector.memset(accd[:, :], 0.0).then_inc(accd_done, 1)
                with dve.Fori(0, CYC_A) as i:
                    n = dve.snap(i + b * CYC_A)
                    g8 = dve.snap(n * GPC)
                    done = dve.snap(adds + i * len(DVE_SUMS))
                    for q in range(GPC):
                        s = q // 2
                        grp_x = xa[:, s, (q % 2) * AG * C:(q % 2 + 1) * AG * C]
                        dve.wait_ge(h_done, g8 + (q + 1))
                        sub = nc.vector.tensor_tensor(hl[:, q % HL, :, C:2 * C], grp_x.rearrange("p (t c) -> p t c", t=AG),
                                                      hl[:, q % HL, :, 0:C], ALU.subtract)
                        sub.then_inc(l_done, 1)
                        if q in DVE_SUMS:
                            k = DVE_SUMS.index(q)
                            dve.wait_ge(accd_done, done + (k + 1))
                            nc.vector.tensor_tensor(accd[:, :], accd[:, :], grp_x, ALU.add).then_inc(accd_done, 1)
                        if q % 2 == 1:
                            dve.wait_ge(l_done, g8 + (q + 1))
                            if q in DVE_SUMS or q - 1 in DVE_SUMS:
                                dve.wait_ge(accd_done, done + (sum(z <= q for z in DVE_SUMS) + 1))
                            dve.sem_inc(xa_free_dve, 1)

            def split_t(g0, g):
                dve.wait_ge(hT_done, g0 + (g + 1))
                sub = nc.vector.tensor_tensor(lT[:, g % HT].rearrange("p k t c -> p (k t c)"), TP[g % TB][:, :],
                                              hT[:, g % HT].rearrange("p k t c -> p (k t c)"), ALU.subtract)
                sub.then_inc(lT_done, 1)

            def evacuate(g0, s16, g):
                c, i = divmod(g, CG)
                if i == 0:
                    dve.wait_ge(stored[c % OB], s16 + 16 * (c // OB + 1))
                dve.wait_ge(o_done, g0 + (g + 1 + HT))
                dst = ob[:, c % OB, 2 * i * C:(2 * i + 2) * C].rearrange("p (t c) -> p t c", t=2)
                nc.vector.tensor_tensor(dst, OP[g % TB][:, :].rearrange("p (t c) -> p t c", t=2),
                                        beta[:, :].rearrange("p (a c) -> p a c", a=1).broadcast_to([P, 2, C]),
                                        ALU.add).then_inc(ob_done, 1)

            def pass_c(b):
                dve.wait_ge(e["ab"], b + 1)
                for g in range(AHEAD):
                    split_t(b * GRAN, g)
                cycles = GRAN // GCYC
                with dve.Fori(0, cycles - 1) as i:
                    g0 = dve.snap(b * GRAN + i * GCYC)
                    s16 = dve.snap(b * (CHUNKS // OB * 16) + i * (XC // OB * 16))
                    for g in range(GCYC):
                        split_t(g0, g + AHEAD)
                        evacuate(g0, s16, g)
                g0 = b * GRAN + (cycles - 1) * GCYC
                s16 = b * (CHUNKS // OB * 16) + (cycles - 1) * (XC // OB * 16)
                for g in range(GCYC):
                    if g + AHEAD < GCYC:
                        split_t(g0, g + AHEAD)
                    evacuate(g0, s16, g)

            def middle(b, n1, filler):
                b16 = dve.snap(b * 2 * UNITS)
                bcm = dve.snap(b * len(CROPMM))
                bns = dve.snap(b * (NS_ITER - 2))
                b0 = dve.snap(b * DVE_LINKS)
                links = [0]

                def link(ins):
                    links[0] += 1
                    ins.then_inc(dve_link, 1)
                    dve.wait_ge(dve_link, b0 + links[0])

                tt, ts, stt = nc.vector.tensor_tensor, nc.vector.tensor_scalar, nc.vector.scalar_tensor_tensor
                cp = nc.vector.tensor_copy

                def diag(dst, ps, junk=0):
                    for k in range(KB):
                        last = nc.vector.tensor_tensor_reduce(out=Tm[:, k, junk:junk + P], in0=ps[k], in1=ident[:, :], scale=1.0,
                                                              scalar=0.0, op0=ALU.mult, op1=ALU.add,
                                                              accum_out=dst[:, k:k + 1])
                    return last

                def spread(cols, n):
                    return tt(dg[:, 0:n].rearrange("p n k c -> p (n k) c"),
                              ident[:, :].rearrange("p (a c) -> p a c", a=1).broadcast_to([P, n * KB, P]),
                              cols.rearrange("p (n a) -> p n a", a=1).broadcast_to([P, n * KB, P]), ALU.mult)

                def assemble(e0n, tn, dn):
                    dve.wait_ge(e[e0n], n1)
                    tt(S[:, 0, :], e0[:, 0:C], e0[:, C:2 * C], ALU.add)
                    link(tt(S[:, 1, P:C], e1[:, 0:P], e1[:, 2 * P:3 * P], ALU.add))
                    dve.wait_ge(e[tn], n1)
                    tt(S[:, 0, :], S[:, 0, :], MB[:, 0:C], ALU.add)
                    tt(S[:, 1, P:C], S[:, 1, P:C], MB[:, C:3 * P], ALU.add).then_inc(e[dn], 1)

                for u in range(UNITS):
                    for k in range(KB):
                        dve.wait_ge(crop_h, b16 + (2 * u + k + 1))
                        cols = slice(u * UROWS, (u + 1) * UROWS)
                        tt(xcT[:, k, 1, :].rearrange("p (j c) -> p j c", j=NJ)[:, :, cols],
                           (MA, MB)[k][:, 0:UPX].rearrange("p (c j) -> p j c", j=NJ),
                           xcT[:, k, 0, :].rearrange("p (j c) -> p j c", j=NJ)[:, :, cols],
                           ALU.subtract).then_inc(crop_l, 1)
                    filler("crop")
                dve.wait_ge(e["gram"], n1)
                cp(e1[:, :], P1[:, 0:3 * P]).then_inc(e["e1"], 1)
                dve.wait_ge(accp_done, (b + 1) * (CYC_A * len(POOL_SUMS) + 1))
                dve.wait_ge(accd_done, (b + 1) * (CYC_A * len(DVE_SUMS) + 1))
                link(tt(accd[:, :], accd[:, :], accp[:, :], ALU.add))
                link(tt(accd[:, 0:2 * C], accd[:, 0:2 * C], accd[:, 2 * C:4 * C], ALU.add))
                tt(accd[:, 0:C], accd[:, 0:C], accd[:, C:2 * C], ALU.add).then_inc(e["acc"], 1)
                filler("gram")
                dve.wait_ge(e["e1"], n1)
                assemble("e0", "tdone", "st")
                filler("assemble")
                dve.wait_ge(e["sbc"], n1)
                dve.wait_ge(e["st"], n1)
                diag(st[:, 0:2], [MA[:, k * P:(k + 1) * P] for k in range(KB)])
                link(diag(st[:, 2:4], [S[:, k, k * P:(k + 1) * P] for k in range(KB)], P))
                ts(st1[:, :], st[:, :], 1.0 / N, None, ALU.mult).then_inc(e["gst"], 1)
                ts(ncc[:, 0, :], st[:, 0:2], -1.0, None, ALU.mult)
                cp(rhs2[:, :, 1], st[:, 0:2])
                filler("mirror")
                dve.wait_ge(e["means"], n1)
                link(cp(gst[:, :], MA[:, 256:260]))
                link(tt(tmp[:, :], gst[:, 0:2], gst[:, 0:2], ALU.mult))
                stt(out=ve[:, :], in0=gst[:, 2:4], scalar=EPS, in1=tmp[:, :], op0=ALU.add,
                    op1=ALU.subtract).then_inc(e["ve"], 1)
                cp(cc[:, 1, :], gst[:, 0:2])
                ts(ncc[:, 1, :], gst[:, 0:2], -1.0, None, ALU.mult)
                ts(rhs2[:, :, 0], gst[:, 0:2], -1.0, None, ALU.mult)
                link(stt(out=cc[:, 2, :], in0=gst[:, 0:2], scalar=-float(N), in1=st[:, 0:2], op0=ALU.mult, op1=ALU.add))
                dve.wait_ge(e["r"], n1)
                spread(cc[:, :, :].rearrange("p n k -> p (n k)"), 3).then_inc(e["dg"], 1)
                filler("stats")
                dve.wait_ge(e["rows"], n1)
                dve.wait_ge(e["s01"], n1)
                for k in range(KB):
                    last = stt(out=Cm[:, k, :], in0=MB[:, C:2 * C], scalar=ncc[:, 0, k:k + 1], in1=S[:, k, :],
                               op0=ALU.mult, op1=ALU.add)
                link(last)
                for k in range(KB):
                    last = stt(out=Cm[:, k, :], in0=MA[:, 0:C], scalar=ncc[:, 1, k:k + 1], in1=Cm[:, k, :],
                               op0=ALU.mult, op1=ALU.add)
                link(last)
                for k in range(KB):
                    last = stt(out=Cm[:, k, :], in0=Cm[:, k, :], scalar=cc[:, 0, k:k + 1], in1=MB[:, 0:C],
                               op0=ALU.mult, op1=ALU.mult)
                link(last)
                link(nc.vector.reduce_max(tmp[:, :], Cm[:, :, :], AX.X))
                ts(nmx[:, :], tmp[:, :], -1.0, None, ALU.mult).then_inc(e["expo"], 1)
                filler("rows")
                dve.wait_ge(e["den"], n1)
                link(nc.vector.reciprocal(tmp[:, :], den[:, :]))
                link(stt(out=acol[:, :], in0=tmp[:, :], scalar=gam[:, 0:1], in1=cc[:, 0, :], op0=ALU.mult, op1=ALU.mult))
                for k in range(KB):
                    last = ts(V[:, k, :], V[:, k, :], acol[:, k:k + 1], None, ALU.mult)
                link(last)
                for k in range(KB):
                    dv = V[:, k, k * P:(k + 1) * P]
                    last = stt(out=dv, in0=ident[:, :], scalar=cc[:, 0, k:k + 1], in1=dv, op0=ALU.mult, op1=ALU.add)
                link(last)
                link(cp(Wm[:, :, :], V[:, :, :]))
                for k in range(KB):
                    dw = Wm[:, k, k * P:(k + 1) * P]
                    last = tt(dw, dw, ident[:, :], ALU.add)
                last.then_inc(e["wdone"], 1)
                filler("scores")
                dve.wait_ge(e["wsp_h"], n1)
                tt(wsp[:, :, 1, :], Wm[:, :, :], wsp[:, :, 0, :], ALU.subtract).then_inc(e["wsp"], 1)
                filler("weights")
                dve.wait_ge(e["proj"], n1)
                pv = MA[:, 0:2 * KB].rearrange("p (k a) -> p k a", a=2)
                cp(bcol[:, :], pv[:, :, 0])
                link(tt(swc[:, :], pv[:, :, 1], st[:, 0:2], ALU.add))
                tt(prod[:, :, :], Wm[:, :, :], MB[:, :].rearrange("p (k c) -> p k c", k=KB), ALU.mult).then_inc(e["prod"], 1)
                link(stt(out=st1[:, 0:2], in0=swc[:, :], scalar=1.0 / N, in1=bcol[:, :], op0=ALU.mult, op1=ALU.add))
                link(stt(out=tmp[:, :], in0=swc[:, :], scalar=1.0 / N, in1=st1[:, 0:2], op0=ALU.mult, op1=ALU.add))
                link(tt(tmp[:, :], tmp[:, :], bcol[:, :], ALU.mult))
                filler("project")
                dve.wait_ge(e["squares"], n1)
                stt(out=st1[:, 2:4], in0=MA[:, 16:18], scalar=1.0 / N, in1=tmp[:, :], op0=ALU.mult,
                    op1=ALU.add).then_inc(e["st1"], 1)
                filler("squares")
                dve.wait_ge(e["gst1"], n1)
                link(cp(gst1[:, :], MA[:, 256:260]))
                link(tt(tmp[:, :], gst1[:, 0:2], gst1[:, 0:2], ALU.mult))
                stt(out=ve[:, :], in0=gst1[:, 2:4], scalar=EPS, in1=tmp[:, :], op0=ALU.add,
                    op1=ALU.subtract).then_inc(e["ve1"], 1)
                link(tt(acol[:, :], bcol[:, :], gst1[:, 0:2], ALU.subtract))
                dve.wait_ge(e["r1"], n1)
                tt(nb1[:, :], acol[:, :], r1[:, :], ALU.mult).then_inc(e["nb1"], 1)
                filler("stats1")
                for i, (jj, m) in enumerate(CROPMM):
                    nj = min(2, NJ - 2 * jj)
                    dve.wait_ge(g_done, bcm + (i + 1 + 2))
                    src = g32[:, i % 2, 0:nj * C].rearrange("p (j c) -> p j c", j=nj)
                    link(cp(ghl[:, m, 2 * jj:2 * jj + nj, 0, :], src))
                    tt(ghl[:, m, 2 * jj:2 * jj + nj, 1, :], src, ghl[:, m, 2 * jj:2 * jj + nj, 0, :],
                       ALU.subtract).then_inc(ghl_done, 1)
                    filler("crop_product")
                dve.wait_ge(e["cov"], n1)
                cp(e1[:, :], P1[:, 0:3 * P]).then_inc(e["e1c"], 1)
                link(cp(Tm[:, 0, :], MA[:, C:2 * C]))
                link(tt(Tm[:, 0, :], Tm[:, 0, :], MA[:, 0:C], ALU.add))
                for k in range(KB):
                    last = nc.vector.tensor_tensor_reduce(out=Tm[:, 1, k * P:(k + 1) * P], in0=Tm[:, 0, k * P:(k + 1) * P],
                                                          in1=ident[:, :], scale=1.0, scalar=0.0, op0=ALU.mult,
                                                          op1=ALU.add, accum_out=sc[:, k:k + 1])
                link(last)
                link(ts(nsc[:, :], sc[:, :], -1.0 / M, None, ALU.mult))
                filler("cov")
                dve.wait_ge(e["e1c"], n1)
                assemble("e0c", "tdonec", "sc")
                filler("cov_assemble")
                dve.wait_ge(e["s01c"], n1)
                dve.wait_ge(e["sc"], n1)
                for k in range(KB):
                    last = stt(out=S[:, k, :], in0=Tm[:, 0, :], scalar=nsc[:, k:k + 1], in1=S[:, k, :],
                               op0=ALU.mult, op1=ALU.add)
                link(last)
                diag(td, [S[:, k, k * P:(k + 1) * P] for k in range(KB)]).then_inc(e["td"], 1)
                filler("cov_mirror")
                dve.wait_ge(e["trps"], n1)
                link(nc.vector.reduce_sum(tr[:, :], MA[:, 256:258], AX.X))
                link(nc.vector.reciprocal(itr[:, :], tr[:, :]))
                link(ts(Cm[:, :, :], S[:, :, :], itr[:, 0:1], None, ALU.mult))
                ts(tr[:, :], tr[:, :], 1.0 / M, None, ALU.mult).then_inc(e["tr"], 1)
                stt(out=YZ[:, :, 1, :], in0=Cm[:, :, :], scalar=-0.5, in1=i15[:, :, :], op0=ALU.mult,
                    op1=ALU.add).then_inc(e["z0"], 1)
                filler("cov_rows")
                filler("trace")
                filler("normal")
                filler("first")
                for i in range(NS_ITER - 2):
                    dve.wait_ge(zy_done, bns + (i + 1))
                    stt(out=Tm[:, :, :], in0=MB[:, :].rearrange("p (k c) -> p k c", k=KB), scalar=-0.5,
                        in1=i15[:, :, :], op0=ALU.mult, op1=ALU.add).then_inc(t_ready, 1)
                    filler("zy")
                    dve.wait_ge(tyz_done, bns + (i + 1))
                    cp(YZ[:, 1].rearrange("p a c -> p (a c)"), MB[:, :]).then_inc(yz_dve, 1)
                    filler("tyz")
                dve.wait_ge(yz_act, bns + (NS_ITER - 2))
                dve.wait_ge(yz_dve, bns + (NS_ITER - 2))
                nc.vector.reduce_sum(v1[:, :], YZ[:, :, 0, :], AX.X).then_inc(e["v1"], 1)
                filler("zv")
                dve.wait_ge(e["zvps"], n1)
                cp(u1[:, :], MA[:, 0:2]).then_inc(e["u1"], 1)
                filler("yu")
                dve.wait_ge(e["yups"], n1)
                dve.wait_ge(e["v1"], n1)
                link(stt(out=tmp[:, :], in0=v1[:, :], scalar=3.0, in1=MA[:, 2:4], op0=ALU.mult, op1=ALU.subtract))
                dve.wait_ge(e["sq"], n1)
                ts(y0[:, :], tmp[:, :], sq[:, 0:1], 0.5 / C, ALU.mult, ALU.mult).then_inc(e["y0c"], 1)
                filler("w1")
                dve.wait_ge(e["w1ps"], n1)
                link(tt(tmp[:, :], MA[:, 4:6], b1c[:, :], ALU.add))
                ts(y1[:, :], tmp[:, :], 0.0, None, ALU.max).then_inc(e["y1"], 1)
                dve.wait_ge(e["w2ps"], n1)
                tt(z2[:, :], MA[:, 6:8], b2c[:, :], ALU.add).then_inc(e["z2"], 1)
                filler("w2")
                dve.wait_ge(e["ez"], n1)
                link(ts(tmp[:, :], ez[:, :], 1.0, None, ALU.add))
                link(nc.vector.reciprocal(y2[:, :], tmp[:, :]))
                link(tt(tmp[:, :], y2[:, :], r1[:, :], ALU.mult))
                ts(ab[:, 0, :], tmp[:, :], 1.0, None, ALU.add)
                link(tt(ez[:, :], tmp[:, :], gst1[:, 0:2], ALU.mult))
                link(tt(tmp[:, :], bcol[:, :], ab[:, 0, :], ALU.mult))
                link(tt(ab[:, 1, :], tmp[:, :], ez[:, :], ALU.subtract))
                spread(ab[:, :, :].rearrange("p n k -> p (n k)"), 2).then_inc(e["dg2"], 1)
                filler("gate")
                dve.wait_ge(e["rows2"], n1)
                tt(prod[:, :, :], Wm[:, :, :], MB[:, 0:C].rearrange("p (a c) -> p a c", a=1).broadcast_to([P, KB, C]),
                   ALU.mult).then_inc(e["wfh"], 1)
                dve.wait_ge(ob_done, b * GRAN + TB)
                cp(beta[:, :], MB[:, C:2 * C])
                dve.wait_ge(e["wf"], n1)
                tt(wf[:, :, 1, :], prod[:, :, :], wf[:, :, 0, :], ALU.subtract).then_inc(e["ab"], 1)
                assert links[0] == DVE_LINKS, links[0]

            def interleaved(b, n1):
                dve.wait_ge(e["ab"], n1)
                g0 = dve.snap(b * GRAN)
                s16 = dve.snap(b * (CHUNKS // OB * 16))
                for g in range(AHEAD):
                    split_t(g0, g)
                at = [0]

                def filler(stage, n=None):
                    for _ in range(dict(STAGES)[stage] if n is None else n):
                        if at[0] + AHEAD < GRAN:
                            split_t(g0, at[0] + AHEAD)
                        evacuate(g0, s16, at[0])
                        at[0] += 1
                return filler

            pass_a(0)
            middle(0, 1, lambda *_: None)
            with dve.Fori(1, B) as b:
                n1 = dve.snap(b + 1)
                pass_a(b)
                filler = interleaved(dve.snap(b - 1), b)
                filler("", GRAN - SPREAD)
                middle(b, n1, filler)
            pass_c(B - 1)

        @block.tensor
        def _(pe):
            mm = nc.tensor.matmul
            pe.wait_ge(pool_const, 4)
            pe.sem_inc(hl_free, HL)
            pe.sem_inc(o_done, HT)
            pe.sem_inc(t_done, GCYC)
            pe.wait_ge(gam_in, 16)
            mm(MA[:, 0:1], onesf[0:1, :], gam0[0:1, 0:1], start=True, stop=True).then_inc(gam_ps, 1)
            pe.wait_ge(gam_ok, 1)

            def zero(ps, n, first, last):
                return mm(ps[:, 0:n], zero16[:, 0:P], zero16[:, 0:n], start=first, stop=last)

            def pass_a(b):
                zero(P0, 2 * C, True, False)
                zero(P1, 3 * P, True, False)
                with pe.Fori(0, CYC_A) as i:
                    g8 = pe.snap(i * GPC + b * (CYC_A * GPC))
                    for q in range(GPC):
                        pe.wait_ge(l_done, g8 + (q + 1))
                        for t in range(AG):
                            h = hl[:, q % HL, t, :]
                            mm(P0[:, :], h[:, 0:P], h, start=False, stop=False)
                            last = mm(P1[:, 0:3 * P], h[:, P:C], h[:, P:2 * C], start=False, stop=False)
                        last.then_inc(hl_free, 1)
                zero(P0, 2 * C, False, True)
                zero(P1, 3 * P, False, True).then_inc(e["gram"], 1)

            def transposes(g0, c16, g):
                c, i = divmod(g, CG)
                if i == 0:
                    pe.wait_ge(xc_in[c % XC], c16 + 16 * (c // XC + 1))
                pe.wait_ge(lT_done, g0 + (g + 1))
                for k in range(KB):
                    for t in range(2):
                        src = xc[:, c % XC, (2 * i + t) * C + k * P:(2 * i + t) * C + (k + 1) * P]
                        last = nc.tensor.transpose(TP[g % TB][:, (2 * k + t) * P:(2 * k + t + 1) * P], src, ident[:, :])
                last.then_inc(t_done, 1)

            def products(g0, g):
                pe.wait_ge(lT_done, g0 + (g + 1 + TB))
                pe.wait_ge(ob_done, g0 + (g + 1))
                for t in range(2):
                    o = OP[g % TB][:, t * C:(t + 1) * C]
                    terms = [(a, k, w) for k in range(KB) for a, w in ((hT, 0), (hT, 1), (lT, 0))]
                    for n, (a, k, w) in enumerate(terms):
                        last = mm(o, a[:, g % HT, k, t, :], wf[:, k, w, :], start=(n == 0), stop=(n + 1 == len(terms)))
                last.then_inc(o_done, 1)

            def c_ready(n1):
                pe.wait_ge(e["ab"], n1)

            def pass_c(b):
                c_ready(b + 1)
                for g in range(AHEAD):
                    transposes(b * GRAN, b * (CHUNKS // XC * 16), g)
                cycles = GRAN // GCYC
                with pe.Fori(0, cycles - 1) as i:
                    g0 = pe.snap(b * GRAN + i * GCYC)
                    c16 = pe.snap(b * (CHUNKS // XC * 16) + i * 16)
                    for g in range(GCYC):
                        transposes(g0, c16, g + AHEAD)
                        products(g0, g)
                g0 = b * GRAN + (cycles - 1) * GCYC
                c16 = b * (CHUNKS // XC * 16) + (cycles - 1) * 16
                for g in range(GCYC):
                    if g + AHEAD < GCYC:
                        transposes(g0, c16, g + AHEAD)
                    products(g0, g)

            def interleaved(b, n1):
                c_ready(n1)
                g0 = pe.snap(b * GRAN)
                c16 = pe.snap(b * (CHUNKS // XC * 16))
                for g in range(AHEAD):
                    transposes(g0, c16, g)
                at = [0]

                def filler(stage, n=None):
                    for _ in range(dict(STAGES)[stage] if n is None else n):
                        if at[0] + AHEAD < GRAN:
                            transposes(g0, c16, at[0] + AHEAD)
                        products(g0, at[0])
                        at[0] += 1
                return filler

            def mat(dst, lhs, rhs, w=C):
                for m in range(KB):
                    for k in range(KB):
                        last = mm(dst(m), lhs(k)[:, m * P:(m + 1) * P], rhs(k), start=(k == 0), stop=(k == KB - 1))
                return last

            def mirror(e0n, e1n, tn, sn, mn, n1, filler, stage, between):
                tr = nc.tensor.transpose
                pe.wait_ge(e[e0n], n1)
                pe.wait_ge(e[e1n], n1)
                tr(MB[:, 0:P], e0[:, C:C + P], ident[:, :])
                tr(MB[:, P:2 * P], e1[:, P:2 * P], ident[:, :])
                tr(MB[:, 2 * P:3 * P], e1[:, 2 * P:3 * P], ident[:, :]).then_inc(e[tn], 1)
                between()
                filler(stage)
                pe.wait_ge(e[sn], n1)
                tr(MB[:, 3 * P:4 * P], S[:, 0, P:C], ident[:, :]).then_inc(e[mn], 1)

            def middle(b, n1, filler):
                b16 = pe.snap(b * 2 * UNITS)
                bcm = pe.snap(b * len(CROPMM))
                bns = pe.snap(b * (NS_ITER - 2))
                pe.wait_ge(crop_in, n1 * 32)
                for u in range(UNITS):
                    for k in range(KB):
                        pe.wait_ge(crop_l, b16 + (2 * u + k + 1))
                        for t in range(UPX // CW):
                            last = nc.tensor.transpose((MA, MB)[k][:, t * CW:(t + 1) * CW],
                                                       xcr[:, u * (UPX // CW) + t, k * P:(k + 1) * P], ident[0:CW, 0:CW])
                        last.then_inc(crop_t, 1)
                    filler("crop")
                filler("gram")
                pe.wait_ge(crop_l, b16 + (2 * UNITS + 2))
                pe.sem_inc(e["crop_free"], 1)

                def channel_sums():
                    pe.wait_ge(e["acc"], n1)
                    mm(MA[:, 0:C], onesf[:, :], accd[:, 0:C], start=True, stop=True).then_inc(e["sbc"], 1)
                mirror("e0", "e1", "tdone", "st", "mirror", n1, filler, "assemble", channel_sums)
                filler("mirror")
                pe.wait_ge(e["gst"], n1)
                mm(MA[:, C:C + 4], grp[:, :], st1[:, :], start=True, stop=True).then_inc(e["means"], 1)
                filler("stats")
                pe.wait_ge(e["dg"], n1)
                pe.wait_ge(e["s01"], n1)
                mm(MB[:, :], onesf[:, :], dg[:, 0:2].rearrange("p n k c -> p (n k c)"), start=True, stop=True)
                mm(MA[:, 0:C], onesf[:, :], dg[:, 2].rearrange("p k c -> p (k c)"), start=True,
                   stop=True).then_inc(e["rows"], 1)
                filler("rows")
                filler("scores")
                pe.wait_ge(e["wdone"], n1)
                mat(lambda m: MA[:, 2 * m:2 * m + 2], lambda k: V[:, k, :], lambda k: rhs2[:, k, :])
                mat(lambda m: MB[:, m * C:(m + 1) * C], lambda k: S[:, k, :], lambda k: Wm[:, k, :]).then_inc(e["proj"], 1)
                filler("weights")
                pe.wait_ge(e["prod"], n1)
                mat(lambda m: MA[:, 16 + m:17 + m], lambda k: prod[:, k, :], lambda k: onesf[:, 0:1]).then_inc(e["squares"], 1)
                filler("project")
                pe.wait_ge(e["st1"], n1)
                mm(MA[:, C:C + 4], grp[:, :], st1[:, :], start=True, stop=True).then_inc(e["gst1"], 1)
                filler("squares")
                filler("stats1")
                pe.wait_ge(e["wsp"], n1)
                pe.wait_ge(e["ve1"], n1)
                for i, (jj, m) in enumerate(CROPMM):
                    c0, n = 2 * jj * C, min(2, NJ - 2 * jj) * C
                    pe.wait_ge(g_done, bcm + (i + 1))
                    terms = [(w, k, a) for k in range(KB) for w, a in ((0, 0), (1, 0), (0, 1))]
                    for j, (w, k, a) in enumerate(terms):
                        last = mm((MA, MB)[m][:, 0:n], wsp[:, k, w, m * P:(m + 1) * P], xcT[:, k, a, c0:c0 + n],
                                  start=(j == 0), stop=(j + 1 == len(terms)))
                    last.then_inc(cm_done, 1)
                    filler("crop_product")
                pe.wait_ge(ghl_done, bcm + (len(CROPMM) + 2))
                pe.wait_ge(g_done, bcm + (len(CROPMM) + 2))
                for i in range(NJ * KB):
                    j, k = divmod(i, KB)
                    g = ghl[:, k, j, :, :].rearrange("p a c -> p (a c)")
                    io = dict(start=(i == 0), stop=(i + 1 == NJ * KB))
                    mm(P0[:, :], g[:, 0:P], g, **io)
                    mm(P1[:, 0:3 * P], g[:, P:C], g[:, P:2 * C], **io)
                    last = mm(MA[:, :], ones16[:, :], g, **io)
                last.then_inc(e["cov"], 1)
                filler("cov")
                mirror("e0c", "e1c", "tdonec", "sc", "mirrorc", n1, filler, "cov_assemble", lambda: None)
                filler("cov_mirror")
                pe.wait_ge(e["td"], n1)
                mm(MA[:, C:C + 2], onesf[:, :], td[:, :], start=True, stop=True).then_inc(e["trps"], 1)
                filler("cov_rows")
                filler("trace")
                pe.wait_ge(e["z0"], n1)
                mat(lambda m: MA[:, m * C:(m + 1) * C], lambda k: Cm[:, k, :], lambda k: YZ[:, k, 1, :]).then_inc(e["y0ps"], 1)
                filler("normal")
                filler("first")
                pe.wait_ge(e["y0"], n1)
                pe.wait_ge(e["s01c"], n1)
                for i in range(NS_ITER - 2):
                    if i:
                        pe.wait_ge(yz_act, bns + i)
                        pe.wait_ge(yz_dve, bns + i)
                    mat(lambda m: MB[:, m * C:(m + 1) * C], lambda k: YZ[:, k, 1, :],
                        lambda k: YZ[:, k, 0, :]).then_inc(zy_done, 1)
                    filler("zy")
                    pe.wait_ge(t_ready, bns + (i + 1))
                    mat(lambda m: (MA, MB)[m][:, :], lambda k: Tm[:, k, :],
                        lambda k: YZ[:, k].rearrange("p a c -> p (a c)")).then_inc(tyz_done, 1)
                    filler("tyz")
                for name, at, lhs, rhs, done, stage in (
                        ("v1", 0, lambda k: YZ[:, k, 1, :], v1, "zvps", "zv"),
                        ("u1", 2, lambda k: YZ[:, k, 0, :], u1, "yups", "yu"),
                        ("y0c", 4, lambda k: w1c[:, k, :], y0, "w1ps", "w1"),
                        ("y1", 6, lambda k: w2c[:, k, :], y1, "w2ps", "w2")):
                    pe.wait_ge(e[name], n1)
                    mat(lambda m: MA[:, at + m:at + m + 1], lhs, lambda k: rhs[:, k:k + 1]).then_inc(e[done], 1)
                    filler(stage)
                pe.wait_ge(e["dg2"], n1)
                mm(MB[:, :], onesf[:, :], dg[:, 0:2].rearrange("p n k c -> p (n k c)"), start=True,
                   stop=True).then_inc(e["rows2"], 1)
                filler("gate")

            pass_a(0)
            middle(0, 1, lambda *_: None)
            with pe.Fori(1, B) as b:
                pass_a(b)
                filler = interleaved(pe.snap(b - 1), b)
                filler("", GRAN - SPREAD)
                middle(b, pe.snap(b + 1), filler)
            pass_c(B - 1)


_INS = ["x", "L0_conv_gamma", "L1_conv_w1", "L1_conv_b1", "L1_conv_w2", "L1_conv_b2"]


def kernel(**inputs):
    import numpy as _np
    import concourse.bacc as _bacc
    from concourse import mybir as _mybir
    from concourse.bass_utils import run_bass_kernel_spmd as _run

    nc = _bacc.Bacc("TRN2", target_bir_lowering=False, num_devices=1)
    arrays, args = {}, []
    for name in _INS:
        a = _np.ascontiguousarray(inputs[name])
        if a.ndim == 0:
            a = a.reshape(1)
        arrays[f"in_{name}"] = a
        args.append(nc.dram_tensor(f"in_{name}", a.shape, _mybir.dt.from_np(a.dtype), kind="ExternalInput").ap())
    args.append(nc.dram_tensor("out_0", (B, H, W_, C), f32, kind="ExternalOutput").ap())
    build(nc, *args)
    r = _run(nc, [arrays], core_ids=[0])
    return r.results[0]["out_0"]
```

```python
import concourse.bass as bass
from concourse import mybir
from contextlib import ExitStack

f32 = mybir.dt.float32
f16 = mybir.dt.float16
ALU = mybir.AluOpType
ACT = mybir.ActivationFunctionType
AX = mybir.AxisListType

B, H, W_, C = 8, 128, 128, 256
N = H * W_
P = 128
KB = C // P
GN = C // 32
CROP = 48
CR0 = (H - CROP) // 2
M = CROP * CROP
NJ = M // C
NS_ITER = 5
EPS = 1e-5

CT = 8
CHUNKS = N // (P * CT)
AG = 4
XA = 4
CYC_A = CHUNKS // XA
GPC = XA * CT // AG
AG_PER_CHUNK = CT // AG
HL = 4
H_AHEAD, L_AHEAD = HL - 1, HL - 2
POOL_SUMS = (0, 1, 3, 4, 6)
DVE_SUMS = tuple(q for q in range(GPC) if q not in POOL_SUMS)

XC = 4
CG = CT // 2
GRAN = CHUNKS * CG
GCYC = XC * CG
TB = 2
HT = 4
OB = 2
AHEAD = 2

CW = 2 * CROP
CTILES = M // CW
UPX = 3 * CW
UNITS = M // UPX
UROWS = UPX // NJ
CROPMM = [(jj, m) for jj in range((NJ + 1) // 2) for m in range(KB)]

FIRST = [("gram", 1), ("assemble", 1), ("mirror", 1)] + [("crop", 1)] * UNITS + [
    ("stats", 2), ("rows", 3), ("scores", 4), ("weights", 3), ("project", 2), ("squares", 2), ("stats1", 3)] + [
    ("crop_product", 1)] * len(CROPMM) + [("cov", 2)]
SECOND = [("cov_assemble", 1), ("cov_mirror", 1), ("trace", 1), ("normal", 1)] + [("zy", 1), ("tyz", 1)] * (NS_ITER - 2) + [
    ("zv", 1), ("yu", 1), ("w1", 1), ("w2", 1), ("gate", 2)]
NAMES = [name for name, _ in FIRST + SECOND]
STEADY = [(c, 0) for _, c in FIRST] + [(0, a) for _, a in SECOND]
A_IN_STEADY = sum(a for _, a in STEADY)
assert A_IN_STEADY % GPC == 0
A_AT = {"crop": 4, "stats": 1, "rows": 1, "scores": 2, "weights": 1, "project": 1, "squares": 1, "stats1": 1,
        "crop_product": 4, "cov": 1, "cov_assemble": 1, "cov_mirror": 1, "trace": 1, "normal": 1,
        "zy": 3, "tyz": 3, "zv": 1, "yu": 1, "w1": 1, "w2": 1, "gate": 1}


def spread(totals):
    plan = []
    for i, name in enumerate(NAMES):
        n, seen, total = NAMES.count(name), NAMES[:i].count(name), totals.get(name, 0)
        plan.append(total * (seen + 1) // n - total * seen // n)
    return plan


OPENING = [(0, a) for a in spread(A_AT)]
assert sum(a for _, a in OPENING) == CYC_A * GPC
CLOSING = [(c, 0) for _, c in FIRST] + [(1, 0)] * (len(SECOND) - 1) + [(0, 0)]
assert max(sum(c for c, _ in plan) for plan in (STEADY, CLOSING)) <= GRAN
DVE_LINKS = 49


def gsums_before(i, j=0):
    n = sum(1 if jj == 0 else min(2, NJ - 2 * jj) for jj, _ in CROPMM[:i])
    return n + j


def filling(plan, c_step, a_step, a_ahead=0):
    at = [0, 0, 0]
    groups = sum(a for _, a in plan)

    def a_run(g):
        if g == 0:
            for first in range(a_ahead):
                a_step(first)
        if g + a_ahead < groups:
            a_step(g + a_ahead)

    def fill(stage):
        assert NAMES[at[0]] == stage, (NAMES[at[0]], stage)
        for kind, step in ((0, c_step), (1, a_run)):
            for _ in range(plan[at[0]][kind]):
                step(at[1 + kind])
                at[1 + kind] += 1
        at[0] += 1
    return fill


def build(nc, x, gamma, w1, b1, w2, b2, out):
    x_chunks = x.rearrange("b h w c -> (b h w) c").rearrange("(n p t) c -> n p (t c)", p=P, t=CT)
    out_chunks = out.rearrange("b h w c -> (b h w) c").rearrange("(n p t) c -> n p (t c)", p=P, t=CT)
    x_crop = x[:, CR0:CR0 + CROP, CR0:CR0 + CROP, :].rearrange("b (t r) w c -> b r w t c", r=2)
    tap = [w[1, 1, :, :].rearrange("(k p) n -> p k n", p=P) for w in (w1, w2)]

    ctx = ExitStack()
    with ctx:
        def sb(name, shape, dt=f32):
            return ctx.enter_context(nc.sbuf_tensor(name, shape, dt))

        def sem(name):
            return ctx.enter_context(nc.semaphore(name))

        xa = sb("xa", [P, XA, CT * C])
        hl = sb("hl", [P, HL, AG, 2 * C], f16)
        accp = sb("accp", [P, AG * C])
        accd = sb("accd", [P, AG * C])
        xc = sb("xc", [P, XC, CT * C])
        hT = sb("hT", [P, HT, 2, 2, P], f16)
        lT = sb("lT", [P, HT, 2, 2, P], f16)
        ob = sb("ob", [P, OB, CT * C])
        wf = sb("wf", [P, KB, 2, C], f16)
        beta = sb("beta", [P, C])
        gsum = sb("gsum", [P, KB, C])
        xcr = sb("xcr", [CW, CTILES, C])
        xcT = sb("xcT", [P, KB, 2, M], f16)
        ghl = sb("ghl", [P, KB, NJ, 2, C], f16)
        g32 = sb("g32", [P, 2, 2 * C])
        S = sb("S", [P, KB, C])
        Cm = sb("Cm", [P, KB, C])
        V = sb("V", [P, KB, C])
        Wm = sb("Wm", [P, KB, C])
        wsp = sb("wsp", [P, KB, 2, C], f16)
        prod = sb("prod", [P, KB, C])
        e0 = prod[:, :, :].rearrange("p k c -> p (k c)")
        YZ = sb("YZ", [P, KB, 2, C])
        e1 = YZ[:, 0, :, :].rearrange("p a c -> p (a c)")[:, 0:3 * P]
        Tm = V
        dg = g32[:, :, :].rearrange("p a (n c) -> p (a n) c", c=P)[:, 0:3 * KB, :].rearrange("p (n k) c -> p n k c", k=KB)
        ident = sb("ident", [P, P])
        i15 = sb("i15", [P, KB, C])
        onesf = sb("onesf", [P, P])
        zero16 = sb("zero16", [P, 2 * C], f16)
        grp = sb("grp", [P, P])
        nhalf = sb("nhalf", [P, KB])
        half = sb("half", [P, 1])
        w1c = sb("w1c", [P, KB, C])
        w2c = sb("w2c", [P, KB, C])
        b1c = sb("b1c", [P, KB])
        b2c = sb("b2c", [P, KB])
        gam0 = sb("gam0", [1, 1])
        gam = sb("gam", [P, 1])
        st = sb("st", [P, 4])
        gst = sb("gst", [P, 4])
        cc = sb("cc", [P, 3, KB])
        ncc = sb("ncc", [P, 2, KB])
        rhs2 = sb("rhs2", [P, KB, 2])
        ve = sb("ve", [P, KB])
        tmp = sb("tmp", [P, KB])
        nmx = sb("nmx", [P, KB])
        den = sb("den", [P, KB])
        acol = sb("acol", [P, KB])
        bcol = sb("bcol", [P, KB])
        swc = sb("swc", [P, KB])
        st1 = sb("st1", [P, 4])
        gst1 = sb("gst1", [P, 4])
        r1 = sb("r1", [P, KB])
        nb1 = sb("nb1", [P, KB])
        sc = sb("sc", [P, KB])
        nsc = sb("nsc", [P, KB])
        td = sb("td", [P, KB])
        tr = sb("tr", [P, 1])
        itr = sb("itr", [P, 1])
        sq = sb("sq", [P, 1])
        v1 = sb("v1", [P, KB])
        u1 = sb("u1", [P, KB])
        y0 = sb("y0", [P, KB])
        y1 = sb("y1", [P, KB])
        z2 = sb("z2", [P, KB])
        ez = sb("ez", [P, KB])
        y2 = sb("y2", [P, KB])
        ab = sb("ab", [P, 2, KB])

        def bank(name):
            return ctx.enter_context(nc.psum_tensor(name, [P, 512], f32))
        P0, P1, MA, MB = bank("P0"), bank("P1"), bank("MA"), bank("MB")
        TP = [bank(f"TP{i}") for i in range(TB)]
        OP = [bank(f"OP{i}") for i in range(TB)]

        def cov_banks(a_of, c_of):
            return (P0, P1) if c_of is not None else (TP[0], TP[1])

        const_in = sem("const_in")
        const_ok = sem("const_ok")
        pool_const = sem("pool_const")
        gam_in, gam_ps, gam_ok = sem("gam_in"), sem("gam_ps"), sem("gam_ok")
        xa_in = [sem(f"xa_in{i}") for i in range(XA)]
        xa_free_pool = sem("xa_free_pool")
        h_done, l_done, hl_free = sem("h_done"), sem("l_done"), sem("hl_free")
        accp_done, accd_done = sem("accp_done"), sem("accd_done")
        xc_in = [sem(f"xc_in{i}") for i in range(XC)]
        t_done, hT_done, lT_done = sem("t_done"), sem("hT_done"), sem("lT_done")
        o_done, even_done, copied, odd_done = sem("o_done"), sem("even_done"), sem("copied"), sem("odd_done")
        stored = [sem(f"stored{i}") for i in range(OB)]
        crop_in, crop_t, crop_h, crop_l = sem("crop_in"), sem("crop_t"), sem("crop_h"), sem("crop_l")
        cm_done, g_done, ghl_done = sem("cm_done"), sem("g_done"), sem("ghl_done")
        gs_done = sem("gs_done")
        dve_link = sem("dve_link")
        tyz_done, yz_act, yz_dve = sem("tyz_done"), sem("yz_act"), sem("yz_dve")
        zy_done, t_ready = sem("zy_done"), sem("t_ready")
        e = {n: sem("e_" + n) for n in (
            "gram e0 e1 tdone s01 mirror acc sbc st gst ve r dg rows means expo den wsp_h wsp wdone proj prod "
            "squares st1 gst1 ve1 r1 nb1 cov e0c e1c tdonec s01c mirrorc td sc trps tr sq z0 y0ps y0 "
            "v1 zvps u1 yups y0c w1ps y1 w2ps z2 ez ab dg2 rows2 wfh wf crop_free").split()}
        block = ctx.enter_context(nc.Block())

        @block.sync
        def _(sp):
            for dst, src in ((w1c, tap[0]), (w2c, tap[1])):
                sp.dma_start(dst[:, :, :], src).then_inc(const_in, 16)
            for dst, src in ((b1c, b1), (b2c, b2)):
                sp.dma_start(dst[:, :], src.rearrange("(k p) -> p k", p=P),
                             allow_slow_non_contiguous=True).then_inc(const_in, 16)
            sp.dma_start(gam0[:, :], gamma.rearrange("(a n) -> a n", a=1)).then_inc(gam_in, 16)

            def load_a(n4, g):
                free = sp.snap(n4 * 2 + 2 * (g + 1))
                sp.wait_ge(l_done, free)
                sp.wait_ge(xa_free_pool, free)
                sp.dma_start(xa[:, g % XA, :], x_chunks[n4 + g]).then_inc(xa_in[g % XA], 16)

            def load_cycles(b, lo, hi):
                with sp.Fori(lo, hi) as i:
                    n4 = sp.snap(b * CHUNKS + i * XA)
                    for s in range(XA):
                        load_a(n4, s)

            def load_crop(b):
                for r in range(2):
                    sp.dma_start(xcr[r * CROP:(r + 1) * CROP, :, :], x_crop[b, r]).then_inc(crop_in, 16)

            def next_crop(b):
                sp.wait_ge(e["crop_free"], b)
                load_crop(b)

            def load_c(b, c):
                sp.wait_ge(t_done, b * GRAN + (c + 1) * CG)
                sp.dma_start(xc[:, c % XC, :], x_chunks[b * CHUNKS + c]).then_inc(xc_in[c % XC], 16)

            def store(b, c):
                complete = sp.snap(b * (GRAN // 2) + ((c + 1) * CG // 2 + 1))
                sp.wait_ge(even_done, complete)
                sp.wait_ge(odd_done, complete)
                sp.dma_start(out_chunks[b * CHUNKS + c], ob[:, c % OB, :]).then_inc(stored[c % OB], 16)

            load_crop(0)
            load_cycles(0, 0, CYC_A)
            load_cycles(1, 0, 1)
            next_crop(1)
            load_cycles(1, 1, CYC_A)
            for c in range(XC):
                load_c(0, c)
            with sp.Fori(1, B - 1) as b:
                bc, ba = sp.snap(b - 1), sp.snap(b + 1)
                for c in range(CHUNKS):
                    if c + XC < CHUNKS:
                        load_c(bc, c + XC)
                    store(bc, c)
                    if c == CHUNKS // 2:
                        for g in range(XA):
                            load_a(ba * CHUNKS, g)
                    if c == CHUNKS * 3 // 4:
                        next_crop(ba)
                for c in range(XC):
                    load_c(b, c)
                load_cycles(ba, 1, CYC_A)
            for b in (B - 2, B - 1):
                for c in range(CHUNKS):
                    if c + XC < CHUNKS:
                        load_c(b, c + XC)
                    elif b + 1 < B:
                        load_c(b + 1, c + XC - CHUNKS)
                    store(b, c)
            for s in range(OB):
                sp.wait_ge(stored[s], 16 * (B * CHUNKS // OB + 1))

        @block.gpsimd
        def _(pool):
            nc.gpsimd.memset(ident[:, :], 0.0)
            nc.gpsimd.memset(grp[:, :], 1.0 / GN)
            nc.gpsimd.memset(onesf[:, :], 1.0)
            nc.gpsimd.memset(nhalf[:, :], -0.5)
            nc.gpsimd.memset(half[:, :], 0.5)
            nc.gpsimd.memset(zero16[:, :], 0.0).then_inc(pool_const, 1)
            pool.wait_ge(pool_const, 1)
            nc.gpsimd.affine_select(out=ident[:, :], in_=ident[:, :], compare_op=ALU.not_equal, fill=1.0,
                                    base=0, pattern=[[-1, P]], channel_multiplier=1).then_inc(pool_const, 1)
            blocks = grp[:, :].rearrange("p (g d) -> p g d", d=GN)
            nc.gpsimd.affine_select(out=blocks, in_=blocks, compare_op=ALU.is_ge, fill=0.0, base=0,
                                    pattern=[[-GN, P // GN], [0, GN]], channel_multiplier=1).then_inc(pool_const, 1)
            pool.wait_ge(pool_const, 3)
            nc.gpsimd.affine_select(out=blocks, in_=blocks, compare_op=ALU.is_ge, fill=0.0, base=GN - 1,
                                    pattern=[[GN, P // GN], [0, GN]], channel_multiplier=-1).then_inc(pool_const, 1)
            pool.sem_inc(xa_free_pool, AG_PER_CHUNK * XA)
            pool.sem_inc(odd_done, 1)

            def add_group(b21, b64, g):
                cyc, q = divmod(g, GPC)
                if q not in POOL_SUMS:
                    return
                k, s = POOL_SUMS.index(q), q // 2
                done = cyc * len(POOL_SUMS) + k + 1
                pool.wait_ge(xa_in[s], b64 + 16 * (cyc + 1))
                pool.wait_ge(accp_done, b21 + done)
                grp_x = xa[:, s, (q % 2) * AG * C:(q % 2 + 1) * AG * C]
                nc.gpsimd.tensor_tensor(accp[:, :], accp[:, :], grp_x, ALU.add).then_inc(accp_done, 1)
                if k + 1 == len(POOL_SUMS) or POOL_SUMS[k + 1] // 2 != s:
                    pool.wait_ge(accp_done, b21 + (done + 1))
                    pool.sem_inc(xa_free_pool, AG_PER_CHUNK)

            def cycles(b, lo, hi):
                with pool.Fori(lo, hi) as i:
                    b21 = pool.snap(b * (CYC_A * len(POOL_SUMS) + 1) + i * len(POOL_SUMS))
                    b64 = pool.snap(b * (CYC_A * 16) + i * 16)
                    for q in range(GPC):
                        add_group(b21, b64, q)

            def add_beta(h0, g):
                if g % 2 == 0:
                    return
                c, i = divmod(g, CG)
                pool.wait_ge(copied, h0 + (g // 2 + 2))
                dst = ob[:, c % OB, 2 * i * C:(2 * i + 2) * C].rearrange("p (t c) -> p t c", t=2)
                nc.gpsimd.tensor_tensor(dst, dst, beta[:, :].rearrange("p (a c) -> p a c", a=1).broadcast_to([P, 2, C]),
                                        ALU.add).then_inc(odd_done, 1)

            def pass_c(b):
                pool.wait_ge(e["ab"], b + 1)
                with pool.Fori(0, GRAN // GCYC) as i:
                    h0 = pool.snap(b * (GRAN // 2) + i * (GCYC // 2))
                    for g in range(GCYC):
                        add_beta(h0, g)

            def middle(b, n1, plan, c_of=None, a_of=None):
                ahead = 0
                if c_of is not None:
                    pool.wait_ge(e["ab"], b)
                    h0 = pool.snap(c_of * (GRAN // 2))
                    ahead = GRAN - sum(c for c, _ in plan)
                for g in range(ahead):
                    add_beta(h0, g)
                bcm = pool.snap(b * len(CROPMM))
                if a_of is not None:
                    b21 = pool.snap(a_of * (CYC_A * len(POOL_SUMS) + 1))
                    b64 = pool.snap(a_of * (CYC_A * 16))
                fill = filling(plan, lambda g: add_beta(h0, g + ahead), lambda g: add_group(b21, b64, g))
                for stage in ["gram", "assemble", "mirror"] + ["crop"] * UNITS:
                    fill(stage)
                pool.wait_ge(e["ve"], n1)
                nc.gpsimd.tensor_tensor(cc[:, 0, :], ve[:, :], nhalf[:, :], ALU.pow).then_inc(e["r"], 1)
                for stage in ("stats", "rows", "scores", "weights", "project", "squares"):
                    fill(stage)
                pool.wait_ge(e["ve1"], n1)
                nc.gpsimd.tensor_tensor(r1[:, :], ve[:, :], nhalf[:, :], ALU.pow).then_inc(e["r1"], 1)
                fill("stats1")
                for i, (jj, m) in enumerate(CROPMM):
                    pool.wait_ge(g_done, bcm + (i + 1 + 2))
                    gs = gsum[:, m, :]
                    for j in range(min(2, NJ - 2 * jj)):
                        src = g32[:, i % 2, j * C:(j + 1) * C]
                        if jj == 0 and j == 0:
                            nc.gpsimd.tensor_tensor(gs, src, g32[:, i % 2, C:2 * C], ALU.add).then_inc(gs_done, 1)
                        elif jj:
                            pool.wait_ge(gs_done, b * (2 * (NJ - 1)) + gsums_before(i, j))
                            nc.gpsimd.tensor_tensor(gs, gs, src, ALU.add).then_inc(gs_done, 1)
                    fill("crop_product")
                fill("cov")
                fill("cov_assemble")
                fill("cov_mirror")
                pool.wait_ge(e["tr"], n1)
                nc.gpsimd.tensor_tensor(sq[:, :], tr[:, :], half[:, :], ALU.pow).then_inc(e["sq"], 1)
                for stage in NAMES[NAMES.index("trace"):]:
                    fill(stage)

            cycles(0, 0, CYC_A)
            middle(0, 1, OPENING, a_of=1)
            with pool.Fori(1, B - 1) as b:
                ba = pool.snap(b + 1)
                middle(b, ba, STEADY, c_of=pool.snap(b - 1), a_of=ba)
                cycles(ba, A_IN_STEADY // GPC, CYC_A)
            middle(B - 1, B, CLOSING, c_of=B - 2)
            pass_c(B - 1)

        @block.scalar
        def _(act):
            act.sem_inc(g_done, 2)
            act.sem_inc(copied, 1)

            def split_group(b32, b64, g):
                cyc, q = divmod(g, GPC)
                s = q // 2
                act.wait_ge(xa_in[s], b64 + 16 * (cyc + 1))
                act.wait_ge(hl_free, b32 + (g + 1))
                src = xa[:, s, (q % 2) * AG * C:(q % 2 + 1) * AG * C].rearrange("p (t c) -> p t c", t=AG)
                nc.scalar.activation(hl[:, q % HL, :, 0:C], src, ACT.Copy).then_inc(h_done, 1)

            def cycles(b, lo, hi):
                with act.Fori(lo, hi) as i:
                    b32 = act.snap(b * (CYC_A * GPC) + i * GPC)
                    b64 = act.snap(b * (CYC_A * 16) + i * 16)
                    for q in range(GPC):
                        split_group(b32, b64, q)

            def split_t(g0, g):
                act.wait_ge(t_done, g0 + (g + 1 + GCYC))
                act.wait_ge(o_done, g0 + (g + 1))
                nc.scalar.activation(hT[:, g % HT].rearrange("p k t c -> p (k t c)"), TP[g % TB][:, :],
                                     ACT.Copy).then_inc(hT_done, 1)

            def evacuate(g0, s16, g):
                if g % 2 == 0:
                    return
                c, i = divmod(g, CG)
                if i == 1:
                    act.wait_ge(stored[c % OB], s16 + 16 * (c // OB + 1))
                act.wait_ge(o_done, g0 + (g + 1 + HT))
                nc.scalar.activation(ob[:, c % OB, 2 * i * C:(2 * i + 2) * C], OP[g % TB][:, :],
                                     ACT.Copy).then_inc(copied, 1)

            def pass_c(b):
                for g in range(AHEAD):
                    split_t(b * GRAN, g)
                cycles = GRAN // GCYC
                with act.Fori(0, cycles - 1) as i:
                    g0 = act.snap(b * GRAN + i * GCYC)
                    s16 = act.snap(b * (CHUNKS // OB * 16) + i * (XC // OB * 16))
                    for g in range(GCYC):
                        split_t(g0, g + AHEAD)
                        evacuate(g0, s16, g)
                g0 = b * GRAN + (cycles - 1) * GCYC
                s16 = b * (CHUNKS // OB * 16) + (cycles - 1) * (XC // OB * 16)
                for g in range(GCYC):
                    if g + AHEAD < GCYC:
                        split_t(g0, g + AHEAD)
                    evacuate(g0, s16, g)

            def middle(b, n1, plan, c_of=None, a_of=None):
                b16 = act.snap(b * 2 * UNITS)
                bcm = act.snap(b * len(CROPMM))
                bns = act.snap(b * (NS_ITER - 2))
                ahead = 0
                if a_of is not None:
                    b32 = act.snap(a_of * (CYC_A * GPC))
                    b64 = act.snap(a_of * (CYC_A * 16))
                if c_of is not None:
                    g0 = act.snap(c_of * GRAN)
                    s16 = act.snap(c_of * (CHUNKS // OB * 16))
                    ahead = GRAN - sum(c for c, _ in plan)
                    for g in range(AHEAD):
                        split_t(g0, g)

                def c_step(g):
                    if g + AHEAD < GRAN:
                        split_t(g0, g + AHEAD)
                    evacuate(g0, s16, g)

                for g in range(ahead):
                    c_step(g)
                filler = filling(plan, lambda g: c_step(g + ahead), lambda g: split_group(b32, b64, g), H_AHEAD)
                act.wait_ge(e["gram"], n1)
                if c_of is not None:
                    act.wait_ge(e["ab"], b)
                nc.scalar.activation(e0[:, :], P0[:, :], ACT.Copy).then_inc(e["e0"], 1)
                filler("gram")
                filler("assemble")
                act.wait_ge(e["mirror"], n1)
                nc.scalar.activation(S[:, 1, 0:P], MB[:, 384:512], ACT.Copy).then_inc(e["s01"], 1)
                filler("mirror")
                for u in range(UNITS):
                    for k in range(KB):
                        act.wait_ge(crop_t, b16 + (2 * u + k + 1))
                        nc.scalar.activation(
                            xcT[:, k, 0, :].rearrange("p (j c) -> p j c", j=NJ)[:, :, u * UROWS:(u + 1) * UROWS],
                            (MA, MB)[k][:, 0:UPX].rearrange("p (c j) -> p j c", j=NJ), ACT.Copy).then_inc(crop_h, 1)
                    filler("crop")
                filler("stats")
                act.wait_ge(e["expo"], n1)
                for k in range(KB):
                    last = nc.scalar.activation(V[:, k, :], Cm[:, k, :], ACT.Exp, bias=nmx[:, k:k + 1],
                                                accum_out=den[:, k:k + 1])
                last.then_inc(e["den"], 1)
                filler("rows")
                act.wait_ge(e["wdone"], n1)
                nc.scalar.activation(wsp[:, :, 0, :], Wm[:, :, :], ACT.Copy).then_inc(e["wsp_h"], 1)
                filler("scores")
                filler("weights")
                filler("project")
                filler("squares")
                act.wait_ge(e["nb1"], n1)
                filler("stats1")
                for i, (jj, m) in enumerate(CROPMM):
                    n = min(2, NJ - 2 * jj) * C
                    act.wait_ge(cm_done, bcm + (i + 1))
                    act.wait_ge(ghl_done, bcm + (i + 1))
                    if i >= 2:
                        act.wait_ge(gs_done, b * (2 * (NJ - 1)) + gsums_before(i - 1))
                    nc.scalar.activation(g32[:, i % 2, 0:n], (MA, MB)[m][:, 0:n], ACT.Identity,
                                         bias=nb1[:, m:m + 1], scale=r1[:, m:m + 1]).then_inc(g_done, 1)
                    filler("crop_product")
                act.wait_ge(e["cov"], n1)
                nc.scalar.activation(e0[:, :], cov_banks(a_of, c_of)[0][:, :], ACT.Copy).then_inc(e["e0c"], 1)
                filler("cov")
                filler("cov_assemble")
                act.wait_ge(e["mirrorc"], n1)
                nc.scalar.activation(S[:, 1, 0:P], MB[:, 384:512], ACT.Copy).then_inc(e["s01c"], 1)
                filler("cov_mirror")
                filler("trace")
                act.wait_ge(e["y0ps"], n1)
                nc.scalar.activation(YZ[:, :, 0, :], MA[:, :].rearrange("p (k c) -> p k c", k=KB),
                                     ACT.Copy).then_inc(e["y0"], 1)
                filler("normal")
                for i in range(NS_ITER - 2):
                    filler("zy")
                    act.wait_ge(tyz_done, bns + (i + 1))
                    nc.scalar.activation(YZ[:, 0].rearrange("p a c -> p (a c)"), MA[:, :], ACT.Copy).then_inc(yz_act, 1)
                    filler("tyz")
                filler("zv")
                filler("yu")
                filler("w1")
                act.wait_ge(e["z2"], n1)
                nc.scalar.activation(ez[:, :], z2[:, :], ACT.Exp, scale=-1.0).then_inc(e["ez"], 1)
                filler("w2")
                act.wait_ge(e["wfh"], n1)
                act.wait_ge(o_done, b * GRAN + HT)
                nc.scalar.activation(wf[:, :, 0, :], prod[:, :, :], ACT.Copy).then_inc(e["wf"], 1)
                filler("gate")

            cycles(0, 0, CYC_A)
            middle(0, 1, OPENING, a_of=1)
            with act.Fori(1, B - 1) as b:
                ba = act.snap(b + 1)
                middle(b, ba, STEADY, c_of=act.snap(b - 1), a_of=ba)
                cycles(ba, A_IN_STEADY // GPC, CYC_A)
            middle(B - 1, B, CLOSING, c_of=B - 2)
            pass_c(B - 1)

        @block.vector
        def _(dve):
            dve.wait_ge(pool_const, 4)
            nc.vector.memset(i15[:, :, :], 0.0).then_inc(const_ok, 1)
            dve.wait_ge(const_ok, 1)
            for k in range(KB):
                last = nc.vector.tensor_scalar(i15[:, k, k * P:(k + 1) * P], ident[:, :], 1.5, None, ALU.mult)
            last.then_inc(const_ok, 1)
            dve.wait_ge(const_ok, 2)
            dve.sem_inc(l_done, AG_PER_CHUNK * XA)
            dve.sem_inc(lT_done, TB)
            dve.sem_inc(even_done, 1)
            dve.sem_inc(ghl_done, 2)
            dve.sem_inc(crop_l, 2)
            for s in range(OB):
                dve.sem_inc(stored[s], 16)
            dve.wait_ge(gam_ps, 1)
            nc.vector.tensor_copy(gam[:, :], MA[:, 0:1]).then_inc(gam_ok, 1)
            dve.wait_ge(gam_ok, 1)
            dve.wait_ge(const_in, 4 * 16)

            def clear_sums():
                nc.vector.memset(accp[:, :], 0.0).then_inc(accp_done, 1)
                nc.vector.memset(accd[:, :], 0.0).then_inc(accd_done, 1)

            def split_group(b32, b64, b13, g):
                cyc, q = divmod(g, GPC)
                s = q // 2
                done = cyc * len(DVE_SUMS) + sum(z < q for z in DVE_SUMS) + 1
                grp_x = xa[:, s, (q % 2) * AG * C:(q % 2 + 1) * AG * C]
                if q in DVE_SUMS:
                    dve.wait_ge(xa_in[s], b64 + 16 * (cyc + 1))
                    dve.wait_ge(accd_done, b13 + done)
                    nc.vector.tensor_tensor(accd[:, :], accd[:, :], grp_x, ALU.add).then_inc(accd_done, 1)
                dve.wait_ge(h_done, b32 + (g + 1))
                nc.vector.tensor_tensor(hl[:, q % HL, :, C:2 * C], grp_x.rearrange("p (t c) -> p t c", t=AG),
                                        hl[:, q % HL, :, 0:C], ALU.subtract).then_inc(l_done, 1)

            def cycles(b, lo, hi):
                with dve.Fori(lo, hi) as i:
                    b32 = dve.snap(b * (CYC_A * GPC) + i * GPC)
                    b64 = dve.snap(b * (CYC_A * 16) + i * 16)
                    b13 = dve.snap(b * (CYC_A * len(DVE_SUMS) + 1) + i * len(DVE_SUMS))
                    for q in range(GPC):
                        split_group(b32, b64, b13, q)

            def split_t(g0, g):
                dve.wait_ge(hT_done, g0 + (g + 1))
                sub = nc.vector.tensor_tensor(lT[:, g % HT].rearrange("p k t c -> p (k t c)"), TP[g % TB][:, :],
                                              hT[:, g % HT].rearrange("p k t c -> p (k t c)"), ALU.subtract)
                sub.then_inc(lT_done, 1)

            def evacuate(g0, s16, g):
                if g % 2:
                    return
                c, i = divmod(g, CG)
                if i == 0:
                    dve.wait_ge(stored[c % OB], s16 + 16 * (c // OB + 1))
                dve.wait_ge(o_done, g0 + (g + 1 + HT))
                dst = ob[:, c % OB, 2 * i * C:(2 * i + 2) * C].rearrange("p (t c) -> p t c", t=2)
                nc.vector.tensor_tensor(dst, OP[g % TB][:, :].rearrange("p (t c) -> p t c", t=2),
                                        beta[:, :].rearrange("p (a c) -> p a c", a=1).broadcast_to([P, 2, C]),
                                        ALU.add).then_inc(even_done, 1)

            def pass_c(b):
                dve.wait_ge(e["ab"], b + 1)
                for g in range(AHEAD):
                    split_t(b * GRAN, g)
                cycles = GRAN // GCYC
                with dve.Fori(0, cycles - 1) as i:
                    g0 = dve.snap(b * GRAN + i * GCYC)
                    s16 = dve.snap(b * (CHUNKS // OB * 16) + i * (XC // OB * 16))
                    for g in range(GCYC):
                        split_t(g0, g + AHEAD)
                        evacuate(g0, s16, g)
                g0 = b * GRAN + (cycles - 1) * GCYC
                s16 = b * (CHUNKS // OB * 16) + (cycles - 1) * (XC // OB * 16)
                for g in range(GCYC):
                    if g + AHEAD < GCYC:
                        split_t(g0, g + AHEAD)
                    evacuate(g0, s16, g)

            def middle(b, n1, plan, c_of=None, a_of=None):
                ahead = 0
                if a_of is not None:
                    b32 = dve.snap(a_of * (CYC_A * GPC))
                    b64 = dve.snap(a_of * (CYC_A * 16))
                    b13 = dve.snap(a_of * (CYC_A * len(DVE_SUMS) + 1))
                if c_of is not None:
                    dve.wait_ge(e["ab"], b)
                    g0 = dve.snap(c_of * GRAN)
                    s16 = dve.snap(c_of * (CHUNKS // OB * 16))
                    ahead = GRAN - sum(c for c, _ in plan)
                    for g in range(AHEAD):
                        split_t(g0, g)

                def c_step(g):
                    if g + AHEAD < GRAN:
                        split_t(g0, g + AHEAD)
                    evacuate(g0, s16, g)

                for g in range(ahead):
                    c_step(g)
                filler = filling(plan, lambda g: c_step(g + ahead), lambda g: split_group(b32, b64, b13, g), L_AHEAD)
                b16 = dve.snap(b * 2 * UNITS)
                bcm = dve.snap(b * len(CROPMM))
                bns = dve.snap(b * (NS_ITER - 2))
                b0 = dve.snap(b * DVE_LINKS)
                links = [0]

                def link(ins):
                    links[0] += 1
                    ins.then_inc(dve_link, 1)
                    dve.wait_ge(dve_link, b0 + links[0])

                tt, ts, stt = nc.vector.tensor_tensor, nc.vector.tensor_scalar, nc.vector.scalar_tensor_tensor
                cp = nc.vector.tensor_copy

                def diag(dst, ps, junk=0):
                    for k in range(KB):
                        last = nc.vector.tensor_tensor_reduce(out=Tm[:, k, junk:junk + P], in0=ps[k], in1=ident[:, :], scale=1.0,
                                                              scalar=0.0, op0=ALU.mult, op1=ALU.add,
                                                              accum_out=dst[:, k:k + 1])
                    return last

                def diagonals(cols, n):
                    return tt(dg[:, 0:n].rearrange("p n k c -> p (n k) c"),
                              ident[:, :].rearrange("p (a c) -> p a c", a=1).broadcast_to([P, n * KB, P]),
                              cols.rearrange("p (n a) -> p n a", a=1).broadcast_to([P, n * KB, P]), ALU.mult)

                def assemble(e0n, tn, dn):
                    dve.wait_ge(e[e0n], n1)
                    tt(S[:, 0, :], e0[:, 0:C], e0[:, C:2 * C], ALU.add)
                    link(tt(S[:, 1, P:C], e1[:, 0:P], e1[:, 2 * P:3 * P], ALU.add))
                    dve.wait_ge(e[tn], n1)
                    tt(S[:, 0, :], S[:, 0, :], MB[:, 0:C], ALU.add)
                    tt(S[:, 1, P:C], S[:, 1, P:C], MB[:, C:3 * P], ALU.add).then_inc(e[dn], 1)

                dve.wait_ge(e["gram"], n1)
                cp(e1[:, :], P1[:, 0:3 * P]).then_inc(e["e1"], 1)
                dve.wait_ge(accp_done, (b + 1) * (CYC_A * len(POOL_SUMS) + 1))
                dve.wait_ge(accd_done, (b + 1) * (CYC_A * len(DVE_SUMS) + 1))
                link(tt(accd[:, :], accd[:, :], accp[:, :], ALU.add))
                link(tt(accd[:, 0:2 * C], accd[:, 0:2 * C], accd[:, 2 * C:4 * C], ALU.add))
                tt(accd[:, 0:C], accd[:, 0:C], accd[:, C:2 * C], ALU.add).then_inc(e["acc"], 1)
                filler("gram")
                dve.wait_ge(e["e1"], n1)
                assemble("e0", "tdone", "st")
                filler("assemble")
                dve.wait_ge(e["sbc"], n1)
                dve.wait_ge(e["st"], n1)
                diag(st[:, 0:2], [MA[:, k * P:(k + 1) * P] for k in range(KB)])
                link(diag(st[:, 2:4], [S[:, k, k * P:(k + 1) * P] for k in range(KB)], P))
                ts(st1[:, :], st[:, :], 1.0 / N, None, ALU.mult).then_inc(e["gst"], 1)
                ts(ncc[:, 0, :], st[:, 0:2], -1.0, None, ALU.mult)
                cp(rhs2[:, :, 1], st[:, 0:2])
                if a_of is not None:
                    clear_sums()
                filler("mirror")
                for u in range(UNITS):
                    for k in range(KB):
                        dve.wait_ge(crop_h, b16 + (2 * u + k + 1))
                        cols = slice(u * UROWS, (u + 1) * UROWS)
                        tt(xcT[:, k, 1, :].rearrange("p (j c) -> p j c", j=NJ)[:, :, cols],
                           (MA, MB)[k][:, 0:UPX].rearrange("p (c j) -> p j c", j=NJ),
                           xcT[:, k, 0, :].rearrange("p (j c) -> p j c", j=NJ)[:, :, cols],
                           ALU.subtract).then_inc(crop_l, 1)
                    filler("crop")
                dve.wait_ge(e["means"], n1)
                link(cp(gst[:, :], MA[:, 256:260]))
                link(tt(tmp[:, :], gst[:, 0:2], gst[:, 0:2], ALU.mult))
                stt(out=ve[:, :], in0=gst[:, 2:4], scalar=EPS, in1=tmp[:, :], op0=ALU.add,
                    op1=ALU.subtract).then_inc(e["ve"], 1)
                cp(cc[:, 1, :], gst[:, 0:2])
                ts(ncc[:, 1, :], gst[:, 0:2], -1.0, None, ALU.mult)
                ts(rhs2[:, :, 0], gst[:, 0:2], -1.0, None, ALU.mult)
                link(stt(out=cc[:, 2, :], in0=gst[:, 0:2], scalar=-float(N), in1=st[:, 0:2], op0=ALU.mult, op1=ALU.add))
                dve.wait_ge(e["r"], n1)
                diagonals(cc[:, :, :].rearrange("p n k -> p (n k)"), 3).then_inc(e["dg"], 1)
                filler("stats")
                dve.wait_ge(e["rows"], n1)
                dve.wait_ge(e["s01"], n1)
                for k in range(KB):
                    last = stt(out=Cm[:, k, :], in0=MB[:, C:2 * C], scalar=ncc[:, 0, k:k + 1], in1=S[:, k, :],
                               op0=ALU.mult, op1=ALU.add)
                link(last)
                for k in range(KB):
                    last = stt(out=Cm[:, k, :], in0=MA[:, 0:C], scalar=ncc[:, 1, k:k + 1], in1=Cm[:, k, :],
                               op0=ALU.mult, op1=ALU.add)
                link(last)
                for k in range(KB):
                    last = stt(out=Cm[:, k, :], in0=Cm[:, k, :], scalar=cc[:, 0, k:k + 1], in1=MB[:, 0:C],
                               op0=ALU.mult, op1=ALU.mult)
                link(last)
                link(nc.vector.reduce_max(tmp[:, :], Cm[:, :, :], AX.X))
                ts(nmx[:, :], tmp[:, :], -1.0, None, ALU.mult).then_inc(e["expo"], 1)
                filler("rows")
                dve.wait_ge(e["den"], n1)
                link(nc.vector.reciprocal(tmp[:, :], den[:, :]))
                link(stt(out=acol[:, :], in0=tmp[:, :], scalar=gam[:, 0:1], in1=cc[:, 0, :], op0=ALU.mult, op1=ALU.mult))
                for k in range(KB):
                    last = ts(V[:, k, :], V[:, k, :], acol[:, k:k + 1], None, ALU.mult)
                link(last)
                for k in range(KB):
                    dv = V[:, k, k * P:(k + 1) * P]
                    last = stt(out=dv, in0=ident[:, :], scalar=cc[:, 0, k:k + 1], in1=dv, op0=ALU.mult, op1=ALU.add)
                link(last)
                link(cp(Wm[:, :, :], V[:, :, :]))
                for k in range(KB):
                    dw = Wm[:, k, k * P:(k + 1) * P]
                    last = tt(dw, dw, ident[:, :], ALU.add)
                last.then_inc(e["wdone"], 1)
                filler("scores")
                dve.wait_ge(e["wsp_h"], n1)
                tt(wsp[:, :, 1, :], Wm[:, :, :], wsp[:, :, 0, :], ALU.subtract).then_inc(e["wsp"], 1)
                dve.wait_ge(e["proj"], n1)
                pv = MA[:, 0:2 * KB].rearrange("p (k a) -> p k a", a=2)
                cp(bcol[:, :], pv[:, :, 0])
                link(tt(swc[:, :], pv[:, :, 1], st[:, 0:2], ALU.add))
                tt(prod[:, :, :], Wm[:, :, :], MB[:, :].rearrange("p (k c) -> p k c", k=KB), ALU.mult).then_inc(e["prod"], 1)
                link(stt(out=st1[:, 0:2], in0=swc[:, :], scalar=1.0 / N, in1=bcol[:, :], op0=ALU.mult, op1=ALU.add))
                link(stt(out=tmp[:, :], in0=swc[:, :], scalar=1.0 / N, in1=st1[:, 0:2], op0=ALU.mult, op1=ALU.add))
                link(tt(tmp[:, :], tmp[:, :], bcol[:, :], ALU.mult))
                filler("weights")
                dve.wait_ge(e["squares"], n1)
                stt(out=st1[:, 2:4], in0=MA[:, 16:18], scalar=1.0 / N, in1=tmp[:, :], op0=ALU.mult,
                    op1=ALU.add).then_inc(e["st1"], 1)
                filler("project")
                dve.wait_ge(e["gst1"], n1)
                link(cp(gst1[:, :], MA[:, 256:260]))
                link(tt(tmp[:, :], gst1[:, 0:2], gst1[:, 0:2], ALU.mult))
                stt(out=ve[:, :], in0=gst1[:, 2:4], scalar=EPS, in1=tmp[:, :], op0=ALU.add,
                    op1=ALU.subtract).then_inc(e["ve1"], 1)
                link(tt(acol[:, :], bcol[:, :], gst1[:, 0:2], ALU.subtract))
                dve.wait_ge(e["r1"], n1)
                tt(nb1[:, :], acol[:, :], r1[:, :], ALU.mult).then_inc(e["nb1"], 1)
                filler("squares")
                filler("stats1")
                for i, (jj, m) in enumerate(CROPMM):
                    nj = min(2, NJ - 2 * jj)
                    dve.wait_ge(g_done, bcm + (i + 1 + 2))
                    src = g32[:, i % 2, 0:nj * C].rearrange("p (j c) -> p j c", j=nj)
                    link(cp(ghl[:, m, 2 * jj:2 * jj + nj, 0, :], src))
                    tt(ghl[:, m, 2 * jj:2 * jj + nj, 1, :], src, ghl[:, m, 2 * jj:2 * jj + nj, 0, :],
                       ALU.subtract).then_inc(ghl_done, 1)
                    filler("crop_product")
                dve.wait_ge(e["cov"], n1)
                cp(e1[:, :], cov_banks(a_of, c_of)[1][:, 0:3 * P]).then_inc(e["e1c"], 1)
                link(cp(Tm[:, 0, :], MA[:, 0:C]))
                for k in range(KB):
                    last = nc.vector.tensor_tensor_reduce(out=Tm[:, 1, k * P:(k + 1) * P], in0=Tm[:, 0, k * P:(k + 1) * P],
                                                          in1=ident[:, :], scale=1.0, scalar=0.0, op0=ALU.mult,
                                                          op1=ALU.add, accum_out=sc[:, k:k + 1])
                link(last)
                link(ts(nsc[:, :], sc[:, :], -1.0 / M, None, ALU.mult))
                filler("cov")
                dve.wait_ge(e["e1c"], n1)
                assemble("e0c", "tdonec", "sc")
                filler("cov_assemble")
                dve.wait_ge(e["s01c"], n1)
                dve.wait_ge(e["sc"], n1)
                for k in range(KB):
                    last = stt(out=S[:, k, :], in0=Tm[:, 0, :], scalar=nsc[:, k:k + 1], in1=S[:, k, :],
                               op0=ALU.mult, op1=ALU.add)
                link(last)
                diag(td, [S[:, k, k * P:(k + 1) * P] for k in range(KB)]).then_inc(e["td"], 1)
                filler("cov_mirror")
                dve.wait_ge(e["trps"], n1)
                link(nc.vector.reduce_sum(tr[:, :], MA[:, 256:258], AX.X))
                link(nc.vector.reciprocal(itr[:, :], tr[:, :]))
                link(ts(Cm[:, :, :], S[:, :, :], itr[:, 0:1], None, ALU.mult))
                ts(tr[:, :], tr[:, :], 1.0 / M, None, ALU.mult).then_inc(e["tr"], 1)
                stt(out=YZ[:, :, 1, :], in0=Cm[:, :, :], scalar=-0.5, in1=i15[:, :, :], op0=ALU.mult,
                    op1=ALU.add).then_inc(e["z0"], 1)
                filler("trace")
                filler("normal")
                for i in range(NS_ITER - 2):
                    dve.wait_ge(zy_done, bns + (i + 1))
                    stt(out=Tm[:, :, :], in0=MB[:, :].rearrange("p (k c) -> p k c", k=KB), scalar=-0.5,
                        in1=i15[:, :, :], op0=ALU.mult, op1=ALU.add).then_inc(t_ready, 1)
                    filler("zy")
                    dve.wait_ge(tyz_done, bns + (i + 1))
                    cp(YZ[:, 1].rearrange("p a c -> p (a c)"), MB[:, :]).then_inc(yz_dve, 1)
                    if i < NS_ITER - 3:
                        filler("tyz")
                dve.wait_ge(yz_act, bns + (NS_ITER - 2))
                dve.wait_ge(yz_dve, bns + (NS_ITER - 2))
                nc.vector.reduce_sum(v1[:, :], YZ[:, :, 0, :], AX.X).then_inc(e["v1"], 1)
                filler("tyz")
                dve.wait_ge(e["zvps"], n1)
                cp(u1[:, :], MA[:, 0:2]).then_inc(e["u1"], 1)
                filler("zv")
                dve.wait_ge(e["yups"], n1)
                dve.wait_ge(e["v1"], n1)
                link(stt(out=tmp[:, :], in0=v1[:, :], scalar=3.0, in1=MA[:, 2:4], op0=ALU.mult, op1=ALU.subtract))
                dve.wait_ge(e["sq"], n1)
                ts(y0[:, :], tmp[:, :], sq[:, 0:1], 0.5 / C, ALU.mult, ALU.mult).then_inc(e["y0c"], 1)
                filler("yu")
                dve.wait_ge(e["w1ps"], n1)
                link(tt(tmp[:, :], MA[:, 4:6], b1c[:, :], ALU.add))
                ts(y1[:, :], tmp[:, :], 0.0, None, ALU.max).then_inc(e["y1"], 1)
                filler("w1")
                dve.wait_ge(e["w2ps"], n1)
                tt(z2[:, :], MA[:, 6:8], b2c[:, :], ALU.add).then_inc(e["z2"], 1)
                dve.wait_ge(e["ez"], n1)
                link(ts(tmp[:, :], ez[:, :], 1.0, None, ALU.add))
                link(nc.vector.reciprocal(y2[:, :], tmp[:, :]))
                link(tt(tmp[:, :], y2[:, :], r1[:, :], ALU.mult))
                ts(ab[:, 0, :], tmp[:, :], 1.0, None, ALU.add)
                link(tt(ez[:, :], tmp[:, :], gst1[:, 0:2], ALU.mult))
                link(tt(tmp[:, :], bcol[:, :], ab[:, 0, :], ALU.mult))
                link(tt(ab[:, 1, :], tmp[:, :], ez[:, :], ALU.subtract))
                diagonals(ab[:, :, :].rearrange("p n k -> p (n k)"), 2).then_inc(e["dg2"], 1)
                filler("w2")
                dve.wait_ge(e["rows2"], n1)
                tt(prod[:, :, :], Wm[:, :, :], MB[:, 0:C].rearrange("p (a c) -> p a c", a=1).broadcast_to([P, KB, C]),
                   ALU.mult).then_inc(e["wfh"], 1)
                dve.wait_ge(even_done, b * (GRAN // 2) + 1)
                dve.wait_ge(odd_done, b * (GRAN // 2) + 1)
                cp(beta[:, :], MB[:, C:2 * C])
                dve.wait_ge(e["wf"], n1)
                tt(wf[:, :, 1, :], prod[:, :, :], wf[:, :, 0, :], ALU.subtract).then_inc(e["ab"], 1)
                filler("gate")
                assert links[0] == DVE_LINKS, links[0]

            clear_sums()
            cycles(0, 0, CYC_A)
            middle(0, 1, OPENING, a_of=1)
            with dve.Fori(1, B - 1) as b:
                ba = dve.snap(b + 1)
                middle(b, ba, STEADY, c_of=dve.snap(b - 1), a_of=ba)
                cycles(ba, A_IN_STEADY // GPC, CYC_A)
            middle(B - 1, B, CLOSING, c_of=B - 2)
            pass_c(B - 1)

        @block.tensor
        def _(pe):
            mm = nc.tensor.matmul
            pe.wait_ge(pool_const, 4)
            pe.sem_inc(hl_free, HL)
            pe.sem_inc(o_done, HT)
            pe.sem_inc(t_done, GCYC)
            pe.wait_ge(gam_in, 16)
            mm(MA[:, 0:1], onesf[0:1, :], gam0[0:1, 0:1], start=True, stop=True).then_inc(gam_ps, 1)
            pe.wait_ge(gam_ok, 1)

            def zero(ps, n, first, last):
                return mm(ps[:, 0:n], zero16[:, 0:P], zero16[:, 0:n], start=first, stop=last)

            def open_gram():
                zero(P0, 2 * C, True, False)
                zero(P1, 3 * P, True, False)

            def close_gram():
                zero(P0, 2 * C, False, True)
                zero(P1, 3 * P, False, True).then_inc(e["gram"], 1)

            def gram_group(b32, g):
                pe.wait_ge(l_done, b32 + (g + 1 + AG_PER_CHUNK * XA))
                for t in range(AG):
                    h = hl[:, g % HL, t, :]
                    mm(P0[:, :], h[:, 0:P], h, start=False, stop=False)
                    last = mm(P1[:, 0:3 * P], h[:, P:C], h[:, P:2 * C], start=False, stop=False)
                last.then_inc(hl_free, 1)

            def cycles(b, lo, hi):
                with pe.Fori(lo, hi) as i:
                    b32 = pe.snap(b * (CYC_A * GPC) + i * GPC)
                    for q in range(GPC):
                        gram_group(b32, q)

            def transposes(g0, c16, g):
                c, i = divmod(g, CG)
                if i == 0:
                    pe.wait_ge(xc_in[c % XC], c16 + 16 * (c // XC + 1))
                pe.wait_ge(lT_done, g0 + (g + 1))
                for k in range(KB):
                    for t in range(2):
                        src = xc[:, c % XC, (2 * i + t) * C + k * P:(2 * i + t) * C + (k + 1) * P]
                        last = nc.tensor.transpose(TP[g % TB][:, (2 * k + t) * P:(2 * k + t + 1) * P], src, ident[:, :])
                last.then_inc(t_done, 1)

            def products(g0, h0, g):
                pe.wait_ge(lT_done, g0 + (g + 1 + TB))
                pe.wait_ge(copied if g % 2 else even_done, h0 + (g // 2 + 1))
                for t in range(2):
                    o = OP[g % TB][:, t * C:(t + 1) * C]
                    terms = [(a, k, w) for k in range(KB) for a, w in ((hT, 0), (hT, 1), (lT, 0))]
                    for n, (a, k, w) in enumerate(terms):
                        last = mm(o, a[:, g % HT, k, t, :], wf[:, k, w, :], start=(n == 0), stop=(n + 1 == len(terms)))
                last.then_inc(o_done, 1)

            def c_ready(n1):
                pe.wait_ge(e["ab"], n1)

            def pass_c(b):
                c_ready(b + 1)
                for g in range(AHEAD):
                    transposes(b * GRAN, b * (CHUNKS // XC * 16), g)
                cycles = GRAN // GCYC
                with pe.Fori(0, cycles - 1) as i:
                    g0 = pe.snap(b * GRAN + i * GCYC)
                    h0 = pe.snap(b * (GRAN // 2) + i * (GCYC // 2))
                    c16 = pe.snap(b * (CHUNKS // XC * 16) + i * 16)
                    for g in range(GCYC):
                        transposes(g0, c16, g + AHEAD)
                        products(g0, h0, g)
                h0 = b * (GRAN // 2) + (cycles - 1) * (GCYC // 2)
                g0 = b * GRAN + (cycles - 1) * GCYC
                c16 = b * (CHUNKS // XC * 16) + (cycles - 1) * 16
                for g in range(GCYC):
                    if g + AHEAD < GCYC:
                        transposes(g0, c16, g + AHEAD)
                    products(g0, h0, g)

            def mat(dst, lhs, rhs, w=C):
                for m in range(KB):
                    for k in range(KB):
                        last = mm(dst(m), lhs(k)[:, m * P:(m + 1) * P], rhs(k), start=(k == 0), stop=(k == KB - 1))
                return last

            def mirror(e0n, e1n, tn, sn, mn, n1, filler, stage, between):
                tr = nc.tensor.transpose
                pe.wait_ge(e[e0n], n1)
                pe.wait_ge(e[e1n], n1)
                tr(MB[:, 0:P], e0[:, C:C + P], ident[:, :])
                tr(MB[:, P:2 * P], e1[:, P:2 * P], ident[:, :])
                tr(MB[:, 2 * P:3 * P], e1[:, 2 * P:3 * P], ident[:, :]).then_inc(e[tn], 1)
                between()
                filler(stage)
                pe.wait_ge(e[sn], n1)
                tr(MB[:, 3 * P:4 * P], S[:, 0, P:C], ident[:, :]).then_inc(e[mn], 1)

            def middle(b, n1, plan, c_of=None, a_of=None):
                ahead = 0
                if a_of is not None:
                    b32 = pe.snap(a_of * (CYC_A * GPC))
                if c_of is not None:
                    c_ready(b)
                    g0 = pe.snap(c_of * GRAN)
                    h0 = pe.snap(c_of * (GRAN // 2))
                    c16 = pe.snap(c_of * (CHUNKS // XC * 16))
                    ahead = GRAN - sum(c for c, _ in plan)
                    for g in range(AHEAD):
                        transposes(g0, c16, g)

                def c_step(g):
                    if g + AHEAD < GRAN:
                        transposes(g0, c16, g + AHEAD)
                    products(g0, h0, g)

                def a_step(g):
                    if g == 0:
                        open_gram()
                    gram_group(b32, g)

                for g in range(ahead):
                    c_step(g)
                filler = filling(plan, lambda g: c_step(g + ahead), a_step)
                b16 = pe.snap(b * 2 * UNITS)
                bcm = pe.snap(b * len(CROPMM))
                bns = pe.snap(b * (NS_ITER - 2))
                filler("gram")

                def channel_sums():
                    pe.wait_ge(e["acc"], n1)
                    mm(MA[:, 0:C], onesf[:, :], accd[:, 0:C], start=True, stop=True).then_inc(e["sbc"], 1)
                mirror("e0", "e1", "tdone", "st", "mirror", n1, filler, "assemble", channel_sums)
                filler("mirror")
                pe.wait_ge(e["gst"], n1)
                pe.wait_ge(e["s01"], n1)
                pe.wait_ge(crop_in, n1 * 32)
                for u in range(UNITS):
                    for k in range(KB):
                        pe.wait_ge(crop_l, b16 + (2 * u + k + 1))
                        for t in range(UPX // CW):
                            last = nc.tensor.transpose((MA, MB)[k][:, t * CW:(t + 1) * CW],
                                                       xcr[:, u * (UPX // CW) + t, k * P:(k + 1) * P], ident[0:CW, 0:CW])
                        last.then_inc(crop_t, 1)
                    filler("crop")
                pe.wait_ge(crop_l, b16 + (2 * UNITS + 2))
                pe.sem_inc(e["crop_free"], 1)
                pe.wait_ge(e["gst"], n1)
                mm(MA[:, C:C + 4], grp[:, :], st1[:, :], start=True, stop=True).then_inc(e["means"], 1)
                filler("stats")
                pe.wait_ge(e["dg"], n1)
                mm(MB[:, :], onesf[:, :], dg[:, 0:2].rearrange("p n k c -> p (n k c)"), start=True, stop=True)
                mm(MA[:, 0:C], onesf[:, :], dg[:, 2].rearrange("p k c -> p (k c)"), start=True,
                   stop=True).then_inc(e["rows"], 1)
                filler("rows")
                filler("scores")
                pe.wait_ge(e["wdone"], n1)
                mat(lambda m: MA[:, 2 * m:2 * m + 2], lambda k: V[:, k, :], lambda k: rhs2[:, k, :])
                mat(lambda m: MB[:, m * C:(m + 1) * C], lambda k: S[:, k, :], lambda k: Wm[:, k, :]).then_inc(e["proj"], 1)
                filler("weights")
                pe.wait_ge(e["prod"], n1)
                mat(lambda m: MA[:, 16 + m:17 + m], lambda k: prod[:, k, :], lambda k: onesf[:, 0:1]).then_inc(e["squares"], 1)
                filler("project")
                pe.wait_ge(e["st1"], n1)
                mm(MA[:, C:C + 4], grp[:, :], st1[:, :], start=True, stop=True).then_inc(e["gst1"], 1)
                filler("squares")
                filler("stats1")
                pe.wait_ge(e["wsp"], n1)
                pe.wait_ge(e["ve1"], n1)
                for i, (jj, m) in enumerate(CROPMM):
                    c0, n = 2 * jj * C, min(2, NJ - 2 * jj) * C
                    pe.wait_ge(g_done, bcm + (i + 1))
                    terms = [(w, k, a) for k in range(KB) for w, a in ((0, 0), (1, 0), (0, 1))]
                    for j, (w, k, a) in enumerate(terms):
                        last = mm((MA, MB)[m][:, 0:n], wsp[:, k, w, m * P:(m + 1) * P], xcT[:, k, a, c0:c0 + n],
                                  start=(j == 0), stop=(j + 1 == len(terms)))
                    last.then_inc(cm_done, 1)
                    filler("crop_product")
                pe.wait_ge(ghl_done, bcm + (len(CROPMM) + 2))
                pe.wait_ge(g_done, bcm + (len(CROPMM) + 2))
                q0, q1 = cov_banks(a_of, c_of)
                for i in range(NJ * KB):
                    j, k = divmod(i, KB)
                    g = ghl[:, k, j, :, :].rearrange("p a c -> p (a c)")
                    io = dict(start=(i == 0), stop=(i + 1 == NJ * KB))
                    mm(q0[:, :], g[:, 0:P], g, **io)
                    mm(q1[:, 0:3 * P], g[:, P:C], g[:, P:2 * C], **io)
                pe.wait_ge(gs_done, n1 * (2 * (NJ - 1)))
                for k in range(KB):
                    last = mm(MA[:, 0:C], onesf[:, :], gsum[:, k, :], start=(k == 0), stop=(k == KB - 1))
                last.then_inc(e["cov"], 1)
                filler("cov")
                mirror("e0c", "e1c", "tdonec", "sc", "mirrorc", n1, filler, "cov_assemble", lambda: None)
                filler("cov_mirror")
                pe.wait_ge(e["td"], n1)
                mm(MA[:, C:C + 2], onesf[:, :], td[:, :], start=True, stop=True).then_inc(e["trps"], 1)
                filler("trace")
                pe.wait_ge(e["z0"], n1)
                mat(lambda m: MA[:, m * C:(m + 1) * C], lambda k: Cm[:, k, :], lambda k: YZ[:, k, 1, :]).then_inc(e["y0ps"], 1)
                filler("normal")
                pe.wait_ge(e["y0"], n1)
                pe.wait_ge(e["s01c"], n1)
                for i in range(NS_ITER - 2):
                    if i:
                        pe.wait_ge(yz_act, bns + i)
                        pe.wait_ge(yz_dve, bns + i)
                    mat(lambda m: MB[:, m * C:(m + 1) * C], lambda k: YZ[:, k, 1, :],
                        lambda k: YZ[:, k, 0, :]).then_inc(zy_done, 1)
                    filler("zy")
                    pe.wait_ge(t_ready, bns + (i + 1))
                    mat(lambda m: (MA, MB)[m][:, :], lambda k: Tm[:, k, :],
                        lambda k: YZ[:, k].rearrange("p a c -> p (a c)")).then_inc(tyz_done, 1)
                    filler("tyz")
                for name, at, lhs, rhs, done, stage in (
                        ("v1", 0, lambda k: YZ[:, k, 1, :], v1, "zvps", "zv"),
                        ("u1", 2, lambda k: YZ[:, k, 0, :], u1, "yups", "yu"),
                        ("y0c", 4, lambda k: w1c[:, k, :], y0, "w1ps", "w1"),
                        ("y1", 6, lambda k: w2c[:, k, :], y1, "w2ps", "w2")):
                    pe.wait_ge(e[name], n1)
                    mat(lambda m: MA[:, at + m:at + m + 1], lhs, lambda k: rhs[:, k:k + 1]).then_inc(e[done], 1)
                    filler(stage)
                pe.wait_ge(e["dg2"], n1)
                mm(MB[:, :], onesf[:, :], dg[:, 0:2].rearrange("p n k c -> p (n k c)"), start=True,
                   stop=True).then_inc(e["rows2"], 1)
                filler("gate")

            open_gram()
            cycles(0, 0, CYC_A)
            close_gram()
            middle(0, 1, OPENING, a_of=1)
            close_gram()
            with pe.Fori(1, B - 1) as b:
                ba = pe.snap(b + 1)
                middle(b, ba, STEADY, c_of=pe.snap(b - 1), a_of=ba)
                cycles(ba, A_IN_STEADY // GPC, CYC_A)
                close_gram()
            middle(B - 1, B, CLOSING, c_of=B - 2)
            pass_c(B - 1)


_INS = ["x", "L0_conv_gamma", "L1_conv_w1", "L1_conv_b1", "L1_conv_w2", "L1_conv_b2"]


def kernel(**inputs):
    import numpy as _np
    import concourse.bacc as _bacc
    from concourse import mybir as _mybir
    from concourse.bass_utils import run_bass_kernel_spmd as _run

    nc = _bacc.Bacc("TRN2", target_bir_lowering=False, num_devices=1)
    arrays, args = {}, []
    for name in _INS:
        a = _np.ascontiguousarray(inputs[name])
        if a.ndim == 0:
            a = a.reshape(1)
        arrays[f"in_{name}"] = a
        args.append(nc.dram_tensor(f"in_{name}", a.shape, _mybir.dt.from_np(a.dtype), kind="ExternalInput").ap())
    args.append(nc.dram_tensor("out_0", (B, H, W_, C), f32, kind="ExternalOutput").ap())
    build(nc, *args)
    r = _run(nc, [arrays], core_ids=[0])
    return r.results[0]["out_0"]
```

```python
import concourse.bass as bass
from concourse import mybir
from contextlib import ExitStack

f32 = mybir.dt.float32
f16 = mybir.dt.float16
ALU = mybir.AluOpType
ACT = mybir.ActivationFunctionType
AX = mybir.AxisListType

B, H, W_, C = 8, 128, 128, 256
N = H * W_
P = 128
KB = C // P
GN = C // 32
CROP = 48
CR0 = (H - CROP) // 2
M = CROP * CROP
NJ = M // C
NS_ITER = 5
EPS = 1e-5

CT = 8
CHUNKS = N // (P * CT)
AG = 4
XA = 4
CYC_A = CHUNKS // XA
GPC = XA * CT // AG
AG_PER_CHUNK = CT // AG
HL = 4
H_AHEAD, L_AHEAD = HL - 1, HL - 2
POOL_ALONE, POOL_BESIDE = (0, 1, 3, 4, 6), (0, 1, 2, 3, 4, 5, 6, 7)
DVE_ALONE, DVE_BESIDE = (tuple(q for q in range(GPC) if q not in pool) for pool in (POOL_ALONE, POOL_BESIDE))

XC = 4
CG = CT // 2
FIRST_LOADS, CROP_LOADS = (3, 6, 7, 10), (11, 14)
GRAN = CHUNKS * CG
GCYC = XC * CG
TB = 2
HT = 4
OB = 2
AHEAD = 2

CW = 2 * CROP
CTILES = M // CW
UPX = 3 * CW
UNITS = M // UPX
UROWS = UPX // NJ
CROPMM = [(jj, m) for jj in range((NJ + 1) // 2) for m in range(KB)]

PAIRS = 4

FIRST = ["gram", "sums", "assemble", "mirror"] + ["crop"] * UNITS + [
    "means", "stats", "rows", "outer", "scores", "maxima", "exp", "softmax", "scale", "matrix", "split", "weights",
    "squares", "stats1"] + ["crop_product"] * len(CROPMM) + ["cov"]
SECOND = ["cov_assemble", "cov_mirror", "trace", "normal"] + ["zy", "tyz"] * (NS_ITER - 3) + [
    "pair"] * PAIRS + ["w1", "alpha", "gate"]
NAMES = FIRST + SECOND
STEADY_C = {"sums": 4, "assemble": 1, "mirror": 2, "crop": 8, "stats": 2, "outer": 1, "scores": 2, "maxima": 1,
            "softmax": 1, "matrix": 1, "split": 1, "weights": 3, "squares": 3, "stats1": 2, "crop_product": 13,
            "cov": 1}
STEADY_A = {"cov_assemble": 1, "cov_mirror": 4, "trace": 2, "normal": 1, "tyz": 4, "pair": 5, "w1": 1, "alpha": 3,
            "gate": 3}
OPENING_A = {"crop": 1, "means": 3, "exp": 1, "softmax": 1, "matrix": 2, "weights": 2, "stats1": 1,
             "crop_product": 4, "cov": 1, "cov_assemble": 2, "cov_mirror": 1, "trace": 1, "normal": 1, "zy": 2,
             "tyz": 2, "pair": 4, "alpha": 2, "gate": 1}
CLOSING_C = {"sums": 1, "assemble": 1, "mirror": 1, "crop": 9, "stats": 2, "scores": 3, "maxima": 2, "exp": 2,
             "scale": 1, "matrix": 2, "split": 2, "weights": 3, "squares": 3, "crop_product": 11, "cov": 3,
             "cov_assemble": 1, "cov_mirror": 2, "trace": 1, "normal": 1, "zy": 2, "tyz": 2, "pair": 4, "alpha": 2}


def spread(totals):
    plan = []
    for i, name in enumerate(NAMES):
        n, seen, total = NAMES.count(name), NAMES[:i].count(name), totals.get(name, 0)
        plan.append(total * (seen + 1) // n - total * seen // n)
    return plan


def all_of_c(totals):
    assert "gram" not in totals and sum(totals.values()) <= GRAN
    return spread({"gram": GRAN - sum(totals.values()), **totals})


STEADY = list(zip(all_of_c(STEADY_C), spread(STEADY_A)))
OPENING = [(0, a) for a in spread(OPENING_A)]
CLOSING = [(c, 0) for c in all_of_c(CLOSING_C)]
A_IN_STEADY = sum(STEADY_A.values())
assert A_IN_STEADY % GPC == 0 and sum(OPENING_A.values()) == CYC_A * GPC
A_CYCLES_BESIDE = A_IN_STEADY // GPC
DVE_LINKS = 50


def adds_before(b, alone, beside):
    steady = A_CYCLES_BESIDE * beside + (CYC_A - A_CYCLES_BESIDE) * alone + 1
    first_two = CYC_A * (alone + beside) + 2
    if isinstance(b, int) and b < 2:
        return b * (CYC_A * alone + 1)
    return b * steady + (first_two - 2 * steady)


def adds_in_cycle(b, i, alone, beside):
    before = adds_before(b, alone, beside) + i * alone
    return before if isinstance(b, int) and b == 0 else before + A_CYCLES_BESIDE * (beside - alone)


def gsums_before(i, j=0):
    n = sum(1 if jj == 0 else min(2, NJ - 2 * jj) for jj, _ in CROPMM[:i])
    return n + j


def filling(plan, c_step, a_step, a_ahead=0):
    at = [0, 0, 0]
    first_a = next((i for i, (_, a) in enumerate(plan) if a), -1)
    assert first_a not in (0, 1)

    def a_run(g):
        if g + a_ahead < CYC_A * GPC:
            a_step(g + a_ahead)

    def fill(stage):
        assert NAMES[at[0]] == stage, (NAMES[at[0]], stage)
        for kind, step in ((0, c_step), (1, a_run)):
            for _ in range(plan[at[0]][kind]):
                step(at[1 + kind])
                at[1 + kind] += 1
        at[0] += 1
        if at[0] == first_a - 1:
            for first in range(a_ahead):
                a_step(first)
    return fill


def build(nc, x, gamma, w1, b1, w2, b2, out):
    x_chunks = x.rearrange("b h w c -> (b h w) c").rearrange("(n p t) c -> n p (t c)", p=P, t=CT)
    out_chunks = out.rearrange("b h w c -> (b h w) c").rearrange("(n p t) c -> n p (t c)", p=P, t=CT)
    x_crop = x[:, CR0:CR0 + CROP, CR0:CR0 + CROP, :].rearrange("b (t r) w c -> b r w t c", r=2)
    tap = [w[1, 1, :, :].rearrange("(k p) n -> p k n", p=P) for w in (w1, w2)]

    ctx = ExitStack()
    with ctx:
        def sb(name, shape, dt=f32):
            return ctx.enter_context(nc.sbuf_tensor(name, shape, dt))

        def sem(name):
            return ctx.enter_context(nc.semaphore(name))

        xa = sb("xa", [P, XA, CT * C])
        hl = sb("hl", [P, HL, AG, 2 * C], f16)
        accp = sb("accp", [P, AG * C])
        accd = sb("accd", [P, AG * C])
        xc = sb("xc", [P, XC, CT * C])
        hT = sb("hT", [P, HT, 2, 2, P], f16)
        lT = sb("lT", [P, HT, 2, 2, P], f16)
        ob = sb("ob", [P, OB, CT * C])
        wf = sb("wf", [P, KB, 2, C], f16)
        beta = sb("beta", [P, C])
        gsum = sb("gsum", [P, KB, C])
        xcr = sb("xcr", [CW, CTILES, C])
        xcT = sb("xcT", [P, KB, 2, M], f16)
        ghl = sb("ghl", [P, KB, NJ, 2, C], f16)
        g32 = sb("g32", [P, 2, 2 * C])
        Sx = sb("Sx", [P, KB, C + 2])
        S, rhs2 = Sx[:, :, 0:C], Sx[:, :, C:C + 2]
        Cm = sb("Cm", [P, KB, C])
        V = sb("V", [P, KB, C])
        Wm = sb("Wm", [P, KB, C])
        wsp = sb("wsp", [P, KB, 2, C], f16)
        prod = sb("prod", [P, KB, C])
        e0 = prod[:, :, :].rearrange("p k c -> p (k c)")
        YZ = sb("YZ", [P, KB, 2, C])
        e1 = YZ[:, 0, :, :].rearrange("p a c -> p (a c)")[:, 0:3 * P]
        Tm = V
        dg = g32[:, :, :].rearrange("p a (n c) -> p (a n) c", c=P)[:, 0:3 * KB, :].rearrange(
            "p (n k) c -> p n k c", k=KB)
        ident = sb("ident", [P, P])
        i15 = sb("i15", [P, KB, C])
        onesf = sb("onesf", [P, P])
        zero16 = sb("zero16", [P, 2 * C], f16)
        grp = sb("grp", [P, P])
        nhalf = sb("nhalf", [P, KB])
        half = sb("half", [P, 1])
        w1c = sb("w1c", [P, KB, C])
        w2r = sb("w2r", [P, KB, C])
        b1r = sb("b1r", [P, C])
        b2c = sb("b2c", [P, KB])
        gam0 = sb("gam0", [1, 1])
        gam = sb("gam", [P, 1])
        st = sb("st", [P, 4])
        gst = sb("gst", [P, 4])
        cc = sb("cc", [P, 3, KB])
        ncc = sb("ncc", [P, 2, KB])
        ve = sb("ve", [P, KB])
        tmp = sb("tmp", [P, KB])
        nmx = sb("nmx", [P, KB])
        den = sb("den", [P, KB])
        acol = sb("acol", [P, KB])
        bcol = sb("bcol", [P, KB])
        proj = sb("proj", [P, KB, 2])
        sqs = sb("sqs", [P, KB])
        st1 = sb("st1", [P, 4])
        gst1 = sb("gst1", [P, 4])
        r1 = sb("r1", [P, KB])
        nb1 = sb("nb1", [P, KB])
        sc = sb("sc", [P, KB])
        nsc = sb("nsc", [P, KB])
        td = sb("td", [P, KB])
        tr = sb("tr", [P, 1])
        itr = sb("itr", [P, 1])
        sq = sb("sq", [P, 1])
        vec = sb("vec", [P, PAIRS + 1, KB])
        z2 = sb("z2", [P, KB])
        ez = sb("ez", [P, KB])
        y2 = sb("y2", [P, KB])
        ab = sb("ab", [P, 2, KB])

        def bank(name):
            return ctx.enter_context(nc.psum_tensor(name, [P, 512], f32))
        P0, P1, MA, MB = bank("P0"), bank("P1"), bank("MA"), bank("MB")
        TP = [bank(f"TP{i}") for i in range(TB)]
        OP = [bank(f"OP{i}") for i in range(TB)]

        def cov_banks(a_of, c_of):
            return (P0, P1) if c_of is not None else (TP[0], TP[1])

        def crop_bank(u, k, c_of):
            return (TP[k] if c_of is None and u % 2 else (MA, MB)[k])

        const_in = sem("const_in")
        const_ok = sem("const_ok")
        pool_const = sem("pool_const")
        gam_in = sem("gam_in")
        w2_ps, w2_ok = sem("w2_ps"), sem("w2_ok")
        xa_in = [sem(f"xa_in{i}") for i in range(XA)]
        xa_free_pool = sem("xa_free_pool")
        h_done, l_done, hl_free = sem("h_done"), sem("l_done"), sem("hl_free")
        accp_done, accd_done, sums_used = sem("accp_done"), sem("accd_done"), sem("sums_used")
        xc_in = [sem(f"xc_in{i}") for i in range(XC)]
        t_done, hT_done, lT_done = sem("t_done"), sem("hT_done"), sem("lT_done")
        o_done, even_done, copied, odd_done = sem("o_done"), sem("even_done"), sem("copied"), sem("odd_done")
        stored = [sem(f"stored{i}") for i in range(OB)]
        crop_in, crop_t, crop_h, crop_l = sem("crop_in"), sem("crop_t"), sem("crop_h"), sem("crop_l")
        cm_done, g32_done, gh_done, ghl_done = sem("cm_done"), sem("g32_done"), sem("gh_done"), sem("ghl_done")
        gs_done = sem("gs_done")
        dve_link = sem("dve_link")
        pair_in, pair_ps = sem("pair_in"), sem("pair_ps")
        tyz_done, yz_act, yz_dve = sem("tyz_done"), sem("yz_act"), sem("yz_dve")
        zy_done, t_ready = sem("zy_done"), sem("t_ready")
        e = {n: sem("e_" + n) for n in (
            "gram e0 e1 tdone s01 mirror acc sbc st gst ve r dg rows means expo den wsp_h wsp wdone wT_ps wT proj "
            "st1 gst1 ve1 r1 nb1 cov e0c e1c tdonec s01c mirrorc td sc trps tr sq z0 y0ps y0 "
            "y0c w1ps z2 ez ab dg2 rows2 wfh wf crop_free").split()}
        block = ctx.enter_context(nc.Block())

        @block.sync
        def _(sp):
            def load_a(n4, g, first=False):
                if not first:
                    free = sp.snap(n4 * 2 + 2 * (g + 1))
                    sp.wait_ge(l_done, free)
                    sp.wait_ge(xa_free_pool, free)
                sp.dma_start(xa[:, g % XA, :], x_chunks[n4 + g]).then_inc(xa_in[g % XA], 16)

            def load_cycles(b, lo, hi):
                with sp.Fori(lo, hi) as i:
                    n4 = sp.snap(b * CHUNKS + i * XA)
                    for s in range(XA):
                        load_a(n4, s)

            def load_crop(b, r):
                if not isinstance(b, int) or b > 0:
                    sp.wait_ge(e["crop_free"], b)
                sp.dma_start(xcr[r * CROP:(r + 1) * CROP, :, :], x_crop[b, r]).then_inc(crop_in, 16)

            def load_c(b, c):
                sp.wait_ge(t_done, b * GRAN + (c + 1) * CG)
                sp.dma_start(xc[:, c % XC, :], x_chunks[b * CHUNKS + c]).then_inc(xc_in[c % XC], 16)

            def store(b, c, parts=1):
                w = CT * C // parts
                for part in range(parts):
                    complete = sp.snap(b * (GRAN // 2) + (c * CG // 2 + (part + 1) * CG // 2 // parts + 1))
                    sp.wait_ge(even_done, complete)
                    sp.wait_ge(odd_done, complete)
                    sp.dma_start(out_chunks[b * CHUNKS + c][:, part * w:(part + 1) * w],
                                 ob[:, c % OB, part * w:(part + 1) * w]).then_inc(stored[c % OB], 16)

            load_a(0, 0, first=True)
            load_a(0, 1, first=True)
            for dst, src in ((prod, tap[1]), (w1c, tap[0])):
                sp.dma_start(dst[:, :, :], src).then_inc(const_in, 16)
            sp.dma_start(b1r[:, :], b1.rearrange("(a n) -> a n", a=1).broadcast_to([P, C])).then_inc(const_in, 16)
            sp.dma_start(b2c[:, :], b2.rearrange("(k p) -> p k", p=P),
                         allow_slow_non_contiguous=True).then_inc(const_in, 16)
            sp.dma_start(gam0[:, :], gamma.rearrange("(a n) -> a n", a=1)).then_inc(gam_in, 16)
            load_a(0, 2, first=True)
            load_a(0, 3, first=True)
            load_cycles(0, 1, CYC_A)
            for r in range(2):
                load_crop(0, r)
            load_cycles(1, 0, 1)
            for r in range(2):
                load_crop(1, r)
            load_cycles(1, 1, CYC_A)
            for c in range(XC):
                load_c(0, c)
            with sp.Fori(1, B - 1) as b:
                bc, ba = sp.snap(b - 1), sp.snap(b + 1)
                for c in range(CHUNKS):
                    if c + XC < CHUNKS:
                        load_c(bc, c + XC)
                    store(bc, c)
                    if c in FIRST_LOADS:
                        load_a(ba * CHUNKS, FIRST_LOADS.index(c))
                    if c in CROP_LOADS:
                        load_crop(ba, CROP_LOADS.index(c))
                load_cycles(ba, 1, 2)
                for s in range(XA):
                    load_a(ba * CHUNKS + 2 * XA, s)
                    load_c(b, s)
                load_cycles(ba, 3, CYC_A)
            for b in (B - 2, B - 1):
                for c in range(CHUNKS):
                    if c + XC < CHUNKS:
                        load_c(b, c + XC)
                    elif b + 1 < B:
                        load_c(b + 1, c + XC - CHUNKS)
                    store(b, c, 2 if (b, c) == (B - 1, CHUNKS - 1) else 1)
            for s in range(OB):
                sp.wait_ge(stored[s], 16 * (B * CHUNKS // OB + 1 + (s == (CHUNKS - 1) % OB)))

        @block.gpsimd
        def _(pool):
            nc.gpsimd.memset(ident[:, :], 0.0)
            nc.gpsimd.memset(grp[:, :], 1.0 / GN)
            nc.gpsimd.memset(onesf[:, :], 1.0)
            nc.gpsimd.memset(nhalf[:, :], -0.5)
            nc.gpsimd.memset(half[:, :], 0.5)
            nc.gpsimd.memset(zero16[:, :], 0.0).then_inc(pool_const, 1)
            pool.wait_ge(pool_const, 1)
            nc.gpsimd.affine_select(out=ident[:, :], in_=ident[:, :], compare_op=ALU.not_equal, fill=1.0,
                                    base=0, pattern=[[-1, P]], channel_multiplier=1).then_inc(pool_const, 1)
            blocks = grp[:, :].rearrange("p (g d) -> p g d", d=GN)
            nc.gpsimd.affine_select(out=blocks, in_=blocks, compare_op=ALU.is_ge, fill=0.0, base=0,
                                    pattern=[[-GN, P // GN], [0, GN]], channel_multiplier=1).then_inc(pool_const, 1)
            pool.wait_ge(pool_const, 3)
            nc.gpsimd.affine_select(out=blocks, in_=blocks, compare_op=ALU.is_ge, fill=0.0, base=GN - 1,
                                    pattern=[[GN, P // GN], [0, GN]], channel_multiplier=-1).then_inc(pool_const, 1)
            pool.sem_inc(xa_free_pool, AG_PER_CHUNK * XA)
            pool.sem_inc(odd_done, 1)

            def clear_sums():
                nc.gpsimd.memset(accp[:, :], 0.0).then_inc(accp_done, 1)
                nc.gpsimd.memset(accd[:, :], 0.0).then_inc(accd_done, 1)

            clear_sums()

            def add_group(before, b64, g, sums):
                cyc, q = divmod(g, GPC)
                if q not in sums:
                    return
                k, s = sums.index(q), q // 2
                done = cyc * len(sums) + k + 1
                pool.wait_ge(xa_in[s], b64 + 16 * (cyc + 1))
                pool.wait_ge(accp_done, before + done)
                grp_x = xa[:, s, (q % 2) * AG * C:(q % 2 + 1) * AG * C]
                nc.gpsimd.tensor_tensor(accp[:, :], accp[:, :], grp_x, ALU.add).then_inc(accp_done, 1)
                if k + 1 == len(sums) or sums[k + 1] // 2 != s:
                    pool.wait_ge(accp_done, before + (done + 1))
                    pool.sem_inc(xa_free_pool, AG_PER_CHUNK)

            def cycles(b, lo, hi):
                with pool.Fori(lo, hi) as i:
                    before = pool.snap(adds_in_cycle(b, i, len(POOL_ALONE), len(POOL_BESIDE)))
                    b64 = pool.snap(b * (CYC_A * 16) + i * 16)
                    for q in range(GPC):
                        add_group(before, b64, q, POOL_ALONE)

            def add_beta(h0, g):
                if g % 2 == 0:
                    return
                c, i = divmod(g, CG)
                pool.wait_ge(copied, h0 + (g // 2 + 2))
                dst = ob[:, c % OB, 2 * i * C:(2 * i + 2) * C].rearrange("p (t c) -> p t c", t=2)
                nc.gpsimd.tensor_tensor(dst, dst, beta[:, :].rearrange("p (a c) -> p a c", a=1).broadcast_to([P, 2, C]),
                                        ALU.add).then_inc(odd_done, 1)

            def pass_c(b):
                pool.wait_ge(e["ab"], b + 1)
                with pool.Fori(0, GRAN // GCYC) as i:
                    h0 = pool.snap(b * (GRAN // 2) + i * (GCYC // 2))
                    for g in range(GCYC):
                        add_beta(h0, g)

            def middle(b, n1, plan, c_of=None, a_of=None):
                if c_of is not None:
                    pool.wait_ge(e["ab"], b)
                    h0 = pool.snap(c_of * (GRAN // 2))
                bcm = pool.snap(b * len(CROPMM))
                if a_of is not None:
                    before = pool.snap(adds_before(a_of, len(POOL_ALONE), len(POOL_BESIDE)))
                    b64 = pool.snap(a_of * (CYC_A * 16))
                fill = filling(plan, lambda g: add_beta(h0, g), lambda g: add_group(before, b64, g, POOL_BESIDE))
                for stage in ("gram", "sums", "assemble"):
                    fill(stage)
                if a_of is not None:
                    pool.wait_ge(e["gst"], n1)
                    pool.sem_inc(sums_used, 1)
                    clear_sums()
                for stage in ["mirror"] + ["crop"] * UNITS:
                    fill(stage)
                pool.wait_ge(e["ve"], n1)
                nc.gpsimd.tensor_tensor(cc[:, 0, :], ve[:, :], nhalf[:, :], ALU.pow).then_inc(e["r"], 1)
                for stage in NAMES[NAMES.index("means"):NAMES.index("squares")]:
                    fill(stage)
                pool.wait_ge(e["ve1"], n1)
                nc.gpsimd.tensor_tensor(r1[:, :], ve[:, :], nhalf[:, :], ALU.pow).then_inc(e["r1"], 1)
                fill("squares")
                fill("stats1")
                for i, (jj, m) in enumerate(CROPMM):
                    pool.wait_ge(g32_done, bcm + (i + 1))
                    gs = gsum[:, m, :]
                    for j in range(min(2, NJ - 2 * jj)):
                        src = g32[:, i % 2, j * C:(j + 1) * C]
                        if jj == 0 and j == 0:
                            nc.gpsimd.tensor_tensor(gs, src, g32[:, i % 2, C:2 * C], ALU.add).then_inc(gs_done, 1)
                        elif jj:
                            pool.wait_ge(gs_done, b * (2 * (NJ - 1)) + gsums_before(i, j))
                            nc.gpsimd.tensor_tensor(gs, gs, src, ALU.add).then_inc(gs_done, 1)
                    fill("crop_product")
                fill("cov")
                fill("cov_assemble")
                fill("cov_mirror")
                pool.wait_ge(e["tr"], n1)
                nc.gpsimd.tensor_tensor(sq[:, :], tr[:, :], half[:, :], ALU.pow).then_inc(e["sq"], 1)
                for stage in NAMES[NAMES.index("trace"):]:
                    fill(stage)

            cycles(0, 0, CYC_A)
            middle(0, 1, OPENING, a_of=1)
            with pool.Fori(1, B - 1) as b:
                ba = pool.snap(b + 1)
                middle(b, ba, STEADY, c_of=pool.snap(b - 1), a_of=ba)
                cycles(ba, A_CYCLES_BESIDE, CYC_A)
            middle(B - 1, B, CLOSING, c_of=B - 2)
            pass_c(B - 1)

        @block.scalar
        def _(act):
            act.sem_inc(gh_done, 2)
            act.sem_inc(copied, 1)

            def split_group(b32, b64, g):
                cyc, q = divmod(g, GPC)
                s = q // 2
                act.wait_ge(xa_in[s], b64 + 16 * (cyc + 1))
                act.wait_ge(hl_free, b32 + (g + 1))
                src = xa[:, s, (q % 2) * AG * C:(q % 2 + 1) * AG * C].rearrange("p (t c) -> p t c", t=AG)
                nc.scalar.activation(hl[:, q % HL, :, 0:C], src, ACT.Copy).then_inc(h_done, 1)

            def cycles(b, lo, hi, ahead):
                def cycle(i, end):
                    b32 = act.snap(b * (CYC_A * GPC) + i * GPC)
                    b64 = act.snap(b * (CYC_A * 16) + i * 16)
                    for q in range(ahead, end):
                        split_group(b32, b64, q)
                if lo < hi - 1:
                    with act.Fori(lo, hi - 1) as i:
                        cycle(i, GPC + ahead)
                cycle(hi - 1, GPC)

            def split_t(g0, g):
                act.wait_ge(t_done, g0 + (g + 1 + GCYC))
                act.wait_ge(o_done, g0 + (g + 1))
                nc.scalar.activation(hT[:, g % HT].rearrange("p k t c -> p (k t c)"), TP[g % TB][:, :],
                                     ACT.Copy).then_inc(hT_done, 1)

            def evacuate(g0, s16, g):
                if g % 2 == 0:
                    return
                c, i = divmod(g, CG)
                if i == 1:
                    act.wait_ge(stored[c % OB], s16 + 16 * (c // OB + 1))
                act.wait_ge(o_done, g0 + (g + 1 + HT))
                nc.scalar.activation(ob[:, c % OB, 2 * i * C:(2 * i + 2) * C], OP[g % TB][:, :],
                                     ACT.Copy).then_inc(copied, 1)

            def pass_c(b):
                for g in range(AHEAD):
                    split_t(b * GRAN, g)
                cycles = GRAN // GCYC
                with act.Fori(0, cycles - 1) as i:
                    g0 = act.snap(b * GRAN + i * GCYC)
                    s16 = act.snap(b * (CHUNKS // OB * 16) + i * (XC // OB * 16))
                    for g in range(GCYC):
                        split_t(g0, g + AHEAD)
                        evacuate(g0, s16, g)
                g0 = b * GRAN + (cycles - 1) * GCYC
                s16 = b * (CHUNKS // OB * 16) + (cycles - 1) * (XC // OB * 16)
                for g in range(GCYC):
                    if g + AHEAD < GCYC:
                        split_t(g0, g + AHEAD)
                    evacuate(g0, s16, g)

            def middle(b, n1, plan, c_of=None, a_of=None):
                b16 = act.snap(b * 2 * UNITS)
                bcm = act.snap(b * len(CROPMM))
                bns = act.snap(b * (NS_ITER - 3))
                if a_of is not None:
                    b32 = act.snap(a_of * (CYC_A * GPC))
                    b64 = act.snap(a_of * (CYC_A * 16))
                if c_of is not None:
                    g0 = act.snap(c_of * GRAN)
                    s16 = act.snap(c_of * (CHUNKS // OB * 16))
                    for g in range(AHEAD):
                        split_t(g0, g)

                def c_step(g):
                    if g + AHEAD < GRAN:
                        split_t(g0, g + AHEAD)
                    evacuate(g0, s16, g)

                filler = filling(plan, c_step, lambda g: split_group(b32, b64, g), H_AHEAD)
                act.wait_ge(e["gram"], n1)
                if c_of is not None:
                    act.wait_ge(e["ab"], b)
                nc.scalar.activation(e0[:, :], P0[:, :], ACT.Copy).then_inc(e["e0"], 1)
                nc.scalar.activation(e1[:, :], P1[:, 0:3 * P], ACT.Copy).then_inc(e["e1"], 1)
                filler("gram")
                filler("sums")
                filler("assemble")
                act.wait_ge(e["mirror"], n1)
                nc.scalar.activation(S[:, 1, 0:P], MB[:, 384:512], ACT.Copy).then_inc(e["s01"], 1)
                filler("mirror")
                for u in range(UNITS):
                    for k in range(KB):
                        act.wait_ge(crop_t, b16 + (2 * u + k + 1))
                        nc.scalar.activation(
                            xcT[:, k, 0, :].rearrange("p (j c) -> p j c", j=NJ)[:, :, u * UROWS:(u + 1) * UROWS],
                            crop_bank(u, k, c_of)[:, 0:UPX].rearrange("p (c j) -> p j c", j=NJ), ACT.Copy).then_inc(crop_h, 1)
                    filler("crop")
                for stage in ("means", "stats", "rows", "outer", "scores", "maxima"):
                    filler(stage)
                act.wait_ge(e["expo"], n1)
                for k in range(KB):
                    last = nc.scalar.activation(V[:, k, :], Cm[:, k, :], ACT.Exp, bias=nmx[:, k:k + 1],
                                                accum_out=den[:, k:k + 1])
                last.then_inc(e["den"], 1)
                for stage in ("exp", "softmax", "scale", "matrix"):
                    filler(stage)
                act.wait_ge(e["wdone"], n1)
                nc.scalar.activation(wsp[:, :, 0, :], Wm[:, :, :], ACT.Copy).then_inc(e["wsp_h"], 1)
                filler("split")
                act.wait_ge(e["wT_ps"], n1)
                nc.scalar.activation(prod[:, :, :].rearrange("p k c -> p (k c)"), cov_banks(a_of, c_of)[1][:, :],
                                     ACT.Copy).then_inc(e["wT"], 1)
                filler("weights")
                filler("squares")
                filler("stats1")
                act.wait_ge(e["nb1"], n1)
                for i, (jj, m) in enumerate(CROPMM):
                    n = min(2, NJ - 2 * jj) * C
                    act.wait_ge(cm_done, bcm + (i + 1))
                    act.wait_ge(ghl_done, bcm + (i + 1))
                    if i >= 2:
                        act.wait_ge(gs_done, b * (2 * (NJ - 1)) + gsums_before(i - 1))
                    nc.scalar.activation(g32[:, i % 2, 0:n], (MA, MB)[m][:, 0:n], ACT.Identity,
                                         bias=nb1[:, m:m + 1], scale=r1[:, m:m + 1]).then_inc(g32_done, 1)
                    nc.scalar.activation(ghl[:, m, 2 * jj:2 * jj + n // C, 0, :],
                                         (MA, MB)[m][:, 0:n].rearrange("p (j c) -> p j c", c=C), ACT.Identity,
                                         bias=nb1[:, m:m + 1], scale=r1[:, m:m + 1]).then_inc(gh_done, 1)
                    filler("crop_product")
                act.wait_ge(e["cov"], n1)
                nc.scalar.activation(e0[:, :], cov_banks(a_of, c_of)[0][:, :], ACT.Copy).then_inc(e["e0c"], 1)
                nc.scalar.activation(e1[:, :], cov_banks(a_of, c_of)[1][:, 0:3 * P], ACT.Copy).then_inc(e["e1c"], 1)
                filler("cov")
                filler("cov_assemble")
                act.wait_ge(e["mirrorc"], n1)
                nc.scalar.activation(S[:, 1, 0:P], MB[:, 384:512], ACT.Copy).then_inc(e["s01c"], 1)
                filler("cov_mirror")
                filler("trace")
                act.wait_ge(e["y0ps"], n1)
                nc.scalar.activation(YZ[:, :, 0, :], MA[:, :].rearrange("p (k c) -> p k c", k=KB),
                                     ACT.Copy).then_inc(e["y0"], 1)
                filler("normal")
                for i in range(NS_ITER - 3):
                    filler("zy")
                    act.wait_ge(tyz_done, bns + (i + 1))
                    nc.scalar.activation(YZ[:, 0].rearrange("p a c -> p (a c)"), MA[:, :], ACT.Copy).then_inc(yz_act, 1)
                    filler("tyz")
                for _ in range(PAIRS):
                    filler("pair")
                act.wait_ge(e["z2"], n1)
                nc.scalar.activation(ez[:, :], z2[:, :], ACT.Exp, scale=-1.0).then_inc(e["ez"], 1)
                filler("w1")
                filler("alpha")
                act.wait_ge(e["wfh"], n1)
                act.wait_ge(o_done, b * GRAN + HT)
                nc.scalar.activation(wf[:, :, 0, :], prod[:, :, :], ACT.Copy).then_inc(e["wf"], 1)
                filler("gate")

            cycles(0, 0, CYC_A, 0)
            act.wait_ge(w2_ps, 1)
            nc.scalar.activation(gam[:, :], MA[:, 0:1], ACT.Copy).then_inc(w2_ok, 1)
            nc.scalar.activation(w2r[:, :, :].rearrange("p k c -> p (k c)"), MB[:, :], ACT.Copy).then_inc(w2_ok, 1)
            middle(0, 1, OPENING, a_of=1)
            with act.Fori(1, B - 1) as b:
                ba = act.snap(b + 1)
                middle(b, ba, STEADY, c_of=act.snap(b - 1), a_of=ba)
                cycles(ba, A_CYCLES_BESIDE, CYC_A, H_AHEAD)
            middle(B - 1, B, CLOSING, c_of=B - 2)
            pass_c(B - 1)

        @block.vector
        def _(dve):
            dve.wait_ge(pool_const, 4)
            nc.vector.memset(i15[:, :, :], 0.0).then_inc(const_ok, 1)
            dve.wait_ge(const_ok, 1)
            for k in range(KB):
                last = nc.vector.tensor_scalar(i15[:, k, k * P:(k + 1) * P], ident[:, :], 1.5, None, ALU.mult)
            last.then_inc(const_ok, 1)
            dve.wait_ge(const_ok, 2)
            dve.sem_inc(l_done, AG_PER_CHUNK * XA)
            dve.sem_inc(lT_done, TB)
            dve.sem_inc(even_done, 1)
            dve.sem_inc(ghl_done, 2)
            dve.sem_inc(crop_l, 2)
            for s in range(OB):
                dve.sem_inc(stored[s], 16)

            def split_group(b32, b64, before, g, sums):
                cyc, q = divmod(g, GPC)
                s = q // 2
                done = cyc * len(sums) + sum(z < q for z in sums) + 1
                grp_x = xa[:, s, (q % 2) * AG * C:(q % 2 + 1) * AG * C]
                if q in sums:
                    dve.wait_ge(xa_in[s], b64 + 16 * (cyc + 1))
                    dve.wait_ge(accd_done, before + done)
                    nc.vector.tensor_tensor(accd[:, :], accd[:, :], grp_x, ALU.add).then_inc(accd_done, 1)
                dve.wait_ge(h_done, b32 + (g + 1))
                nc.vector.tensor_tensor(hl[:, q % HL, :, C:2 * C], grp_x.rearrange("p (t c) -> p t c", t=AG),
                                        hl[:, q % HL, :, 0:C], ALU.subtract).then_inc(l_done, 1)

            def cycles(b, lo, hi, ahead):
                def cycle(i, end):
                    b32 = dve.snap(b * (CYC_A * GPC) + i * GPC)
                    b64 = dve.snap(b * (CYC_A * 16) + i * 16)
                    before = dve.snap(adds_in_cycle(b, i, len(DVE_ALONE), len(DVE_BESIDE)))
                    for q in range(ahead, end):
                        split_group(b32, b64, before, q, DVE_ALONE)
                if lo < hi - 1:
                    with dve.Fori(lo, hi - 1) as i:
                        cycle(i, GPC + ahead)
                cycle(hi - 1, GPC)

            def split_t(g0, g):
                dve.wait_ge(hT_done, g0 + (g + 1))
                sub = nc.vector.tensor_tensor(lT[:, g % HT].rearrange("p k t c -> p (k t c)"), TP[g % TB][:, :],
                                              hT[:, g % HT].rearrange("p k t c -> p (k t c)"), ALU.subtract)
                sub.then_inc(lT_done, 1)

            def evacuate(g0, s16, g):
                if g % 2:
                    return
                c, i = divmod(g, CG)
                if i == 0:
                    dve.wait_ge(stored[c % OB], s16 + 16 * (c // OB + 1))
                dve.wait_ge(o_done, g0 + (g + 1 + HT))
                dst = ob[:, c % OB, 2 * i * C:(2 * i + 2) * C].rearrange("p (t c) -> p t c", t=2)
                nc.vector.tensor_tensor(dst, OP[g % TB][:, :].rearrange("p (t c) -> p t c", t=2),
                                        beta[:, :].rearrange("p (a c) -> p a c", a=1).broadcast_to([P, 2, C]),
                                        ALU.add).then_inc(even_done, 1)

            def pass_c(b):
                dve.wait_ge(e["ab"], b + 1)
                for g in range(AHEAD):
                    split_t(b * GRAN, g)
                cycles = GRAN // GCYC
                with dve.Fori(0, cycles - 1) as i:
                    g0 = dve.snap(b * GRAN + i * GCYC)
                    s16 = dve.snap(b * (CHUNKS // OB * 16) + i * (XC // OB * 16))
                    for g in range(GCYC):
                        split_t(g0, g + AHEAD)
                        evacuate(g0, s16, g)
                g0 = b * GRAN + (cycles - 1) * GCYC
                s16 = b * (CHUNKS // OB * 16) + (cycles - 1) * (XC // OB * 16)
                for g in range(GCYC):
                    if g + AHEAD < GCYC:
                        split_t(g0, g + AHEAD)
                    evacuate(g0, s16, g)

            def middle(b, n1, plan, c_of=None, a_of=None):
                if a_of is not None:
                    b32 = dve.snap(a_of * (CYC_A * GPC))
                    b64 = dve.snap(a_of * (CYC_A * 16))
                    before = dve.snap(adds_before(a_of, len(DVE_ALONE), len(DVE_BESIDE)))
                    before_alone = dve.snap(adds_in_cycle(a_of, 0, len(DVE_ALONE), len(DVE_BESIDE)))
                if c_of is not None:
                    dve.wait_ge(e["ab"], b)
                    g0 = dve.snap(c_of * GRAN)
                    s16 = dve.snap(c_of * (CHUNKS // OB * 16))
                    for g in range(AHEAD):
                        split_t(g0, g)

                def c_step(g):
                    if g + AHEAD < GRAN:
                        split_t(g0, g + AHEAD)
                    evacuate(g0, s16, g)

                def a_step(g):
                    if g < sum(a for _, a in plan):
                        split_group(b32, b64, before, g, DVE_BESIDE)
                    else:
                        split_group(b32, b64, before_alone, g, DVE_ALONE)

                filler = filling(plan, c_step, a_step, L_AHEAD)
                b16 = dve.snap(b * 2 * UNITS)
                bcm = dve.snap(b * len(CROPMM))
                bns = dve.snap(b * (NS_ITER - 3))
                bpair = dve.snap(b * PAIRS)
                b0 = dve.snap(b * DVE_LINKS)
                links = [0]

                def link(ins):
                    links[0] += 1
                    ins.then_inc(dve_link, 1)
                    dve.wait_ge(dve_link, b0 + links[0])

                tt, ts, stt = nc.vector.tensor_tensor, nc.vector.tensor_scalar, nc.vector.scalar_tensor_tensor
                cp = nc.vector.tensor_copy

                def row_products(dst, row, matrix, junk):
                    return nc.vector.tensor_tensor_reduce(out=junk, in0=row, in1=matrix, scale=1.0, scalar=0.0,
                                                          op0=ALU.mult, op1=ALU.add, accum_out=dst)

                def diag(dst, ps, junk=0):
                    for k in range(KB):
                        last = row_products(dst[:, k:k + 1], ps[k], ident[:, :], Tm[:, k, junk:junk + P])
                    return last

                def stationary(cols):
                    return tt(dg[:, 2], onesf[:, :].rearrange("p (a c) -> p a c", a=1).broadcast_to([P, KB, P]),
                              cols.rearrange("p (n a) -> p n a", a=1).broadcast_to([P, KB, P]), ALU.mult)

                def diagonals(cols, n):
                    return tt(dg[:, 0:n].rearrange("p n k c -> p (n k) c"),
                              ident[:, :].rearrange("p (a c) -> p a c", a=1).broadcast_to([P, n * KB, P]),
                              cols.rearrange("p (n a) -> p n a", a=1).broadcast_to([P, n * KB, P]), ALU.mult)

                def assemble(e0n, tn, dn):
                    dve.wait_ge(e[e0n], n1)
                    tt(S[:, 0, :], e0[:, 0:C], e0[:, C:2 * C], ALU.add)
                    link(tt(S[:, 1, P:C], e1[:, 0:P], e1[:, 2 * P:3 * P], ALU.add))
                    dve.wait_ge(e[tn], n1)
                    tt(S[:, 0, :], S[:, 0, :], MB[:, 0:C], ALU.add)
                    tt(S[:, 1, P:C], S[:, 1, P:C], MB[:, C:3 * P], ALU.add).then_inc(e[dn], 1)

                dve.wait_ge(accp_done, adds_before(n1, len(POOL_ALONE), len(POOL_BESIDE)))
                dve.wait_ge(accd_done, adds_before(n1, len(DVE_ALONE), len(DVE_BESIDE)))
                link(tt(accd[:, :], accd[:, :], accp[:, :], ALU.add))
                filler("gram")
                link(tt(accd[:, 0:2 * C], accd[:, 0:2 * C], accd[:, 2 * C:4 * C], ALU.add))
                tt(accd[:, 0:C], accd[:, 0:C], accd[:, C:2 * C], ALU.add).then_inc(e["acc"], 1)
                filler("sums")
                dve.wait_ge(e["e1"], n1)
                assemble("e0", "tdone", "st")
                filler("assemble")
                dve.wait_ge(e["sbc"], n1)
                dve.wait_ge(e["st"], n1)
                diag(st[:, 0:2], [MA[:, k * P:(k + 1) * P] for k in range(KB)])
                link(diag(st[:, 2:4], [S[:, k, k * P:(k + 1) * P] for k in range(KB)], P))
                ts(st1[:, :], st[:, :], 1.0 / N, None, ALU.mult).then_inc(e["gst"], 1)
                ts(ncc[:, 0, :], st[:, 0:2], -1.0, None, ALU.mult)
                cp(rhs2[:, :, 1], st[:, 0:2])
                filler("mirror")
                for u in range(UNITS):
                    for k in range(KB):
                        dve.wait_ge(crop_h, b16 + (2 * u + k + 1))
                        cols = slice(u * UROWS, (u + 1) * UROWS)
                        tt(xcT[:, k, 1, :].rearrange("p (j c) -> p j c", j=NJ)[:, :, cols],
                           crop_bank(u, k, c_of)[:, 0:UPX].rearrange("p (c j) -> p j c", j=NJ),
                           xcT[:, k, 0, :].rearrange("p (j c) -> p j c", j=NJ)[:, :, cols],
                           ALU.subtract).then_inc(crop_l, 1)
                    filler("crop")
                dve.wait_ge(e["means"], n1)
                link(cp(gst[:, :], MA[:, 256:260]))
                link(tt(tmp[:, :], gst[:, 0:2], gst[:, 0:2], ALU.mult))
                stt(out=ve[:, :], in0=gst[:, 2:4], scalar=EPS, in1=tmp[:, :], op0=ALU.add,
                    op1=ALU.subtract).then_inc(e["ve"], 1)
                cp(cc[:, 1, :], gst[:, 0:2])
                ts(ncc[:, 1, :], gst[:, 0:2], -1.0, None, ALU.mult)
                ts(rhs2[:, :, 0], gst[:, 0:2], -1.0, None, ALU.mult)
                link(stt(out=cc[:, 2, :], in0=gst[:, 0:2], scalar=-float(N), in1=st[:, 0:2], op0=ALU.mult, op1=ALU.add))
                filler("means")
                dve.wait_ge(e["r"], n1)
                diagonals(cc[:, :, :].rearrange("p n k -> p (n k)"), 3).then_inc(e["dg"], 1)
                filler("stats")
                dve.wait_ge(e["rows"], n1)
                dve.wait_ge(e["s01"], n1)
                for k in range(KB):
                    last = stt(out=Cm[:, k, :], in0=MB[:, C:2 * C], scalar=ncc[:, 0, k:k + 1], in1=S[:, k, :],
                               op0=ALU.mult, op1=ALU.add)
                link(last)
                filler("rows")
                for k in range(KB):
                    last = stt(out=Cm[:, k, :], in0=MA[:, 0:C], scalar=ncc[:, 1, k:k + 1], in1=Cm[:, k, :],
                               op0=ALU.mult, op1=ALU.add)
                link(last)
                filler("outer")
                for k in range(KB):
                    last = stt(out=Cm[:, k, :], in0=Cm[:, k, :], scalar=cc[:, 0, k:k + 1], in1=MB[:, 0:C],
                               op0=ALU.mult, op1=ALU.mult)
                link(last)
                filler("scores")
                link(nc.vector.reduce_max(tmp[:, :], Cm[:, :, :], AX.X))
                ts(nmx[:, :], tmp[:, :], -1.0, None, ALU.mult).then_inc(e["expo"], 1)
                filler("maxima")
                filler("exp")
                dve.wait_ge(e["den"], n1)
                link(nc.vector.reciprocal(tmp[:, :], den[:, :]))
                link(stt(out=acol[:, :], in0=tmp[:, :], scalar=gam[:, 0:1], in1=cc[:, 0, :], op0=ALU.mult, op1=ALU.mult))
                for k in range(KB):
                    last = ts(V[:, k, :], V[:, k, :], acol[:, k:k + 1], None, ALU.mult)
                link(last)
                filler("softmax")
                for k in range(KB):
                    dv = V[:, k, k * P:(k + 1) * P]
                    last = stt(out=dv, in0=ident[:, :], scalar=cc[:, 0, k:k + 1], in1=dv, op0=ALU.mult, op1=ALU.add)
                link(last)
                filler("scale")
                link(cp(Wm[:, :, :], V[:, :, :]))
                for k in range(KB):
                    dw = Wm[:, k, k * P:(k + 1) * P]
                    last = tt(dw, dw, ident[:, :], ALU.add)
                last.then_inc(e["wdone"], 1)
                filler("matrix")
                filler("split")
                dve.wait_ge(e["wsp_h"], n1)
                tt(wsp[:, :, 1, :], Wm[:, :, :], wsp[:, :, 0, :], ALU.subtract).then_inc(e["wsp"], 1)
                dve.wait_ge(e["proj"], n1)
                for k in range(KB):
                    last = cp(proj[:, k, :], (MA, MB)[k][:, C:C + 2])
                link(last)
                link(tt(bcol[:, :], proj[:, :, 0], gst[:, 0:2], ALU.add))
                link(stt(out=st1[:, 0:2], in0=proj[:, :, 1], scalar=1.0 / N, in1=bcol[:, :], op0=ALU.mult, op1=ALU.add))
                link(stt(out=tmp[:, :], in0=proj[:, :, 1], scalar=1.0 / N, in1=st1[:, 0:2], op0=ALU.mult, op1=ALU.add))
                link(tt(tmp[:, :], tmp[:, :], bcol[:, :], ALU.mult))
                dve.wait_ge(e["wT"], n1)
                for k in range(KB):
                    last = row_products(sqs[:, k:k + 1], (MA, MB)[k][:, 0:C], prod[:, k, :], YZ[:, k, 1, :])
                link(last)
                stt(out=st1[:, 2:4], in0=sqs[:, :], scalar=1.0 / N, in1=tmp[:, :], op0=ALU.mult,
                    op1=ALU.add).then_inc(e["st1"], 1)
                filler("weights")
                dve.wait_ge(e["gst1"], n1)
                link(cp(gst1[:, :], MA[:, 256:260]))
                link(tt(tmp[:, :], gst1[:, 0:2], gst1[:, 0:2], ALU.mult))
                stt(out=ve[:, :], in0=gst1[:, 2:4], scalar=EPS, in1=tmp[:, :], op0=ALU.add,
                    op1=ALU.subtract).then_inc(e["ve1"], 1)
                link(tt(acol[:, :], bcol[:, :], gst1[:, 0:2], ALU.subtract))
                filler("squares")
                dve.wait_ge(e["r1"], n1)
                tt(nb1[:, :], acol[:, :], r1[:, :], ALU.mult).then_inc(e["nb1"], 1)
                filler("stats1")
                for i, (jj, m) in enumerate(CROPMM):
                    nj = min(2, NJ - 2 * jj)
                    src = g32[:, i % 2, 0:nj * C].rearrange("p (j c) -> p j c", j=nj)
                    dve.wait_ge(g32_done, bcm + (i + 1))
                    dve.wait_ge(gh_done, bcm + (i + 1 + 2))
                    tt(ghl[:, m, 2 * jj:2 * jj + nj, 1, :], src, ghl[:, m, 2 * jj:2 * jj + nj, 0, :],
                       ALU.subtract).then_inc(ghl_done, 1)
                    filler("crop_product")
                dve.wait_ge(e["cov"], n1)
                link(diag(sc, [MA[:, k * P:(k + 1) * P] for k in range(KB)]))
                link(ts(nsc[:, :], sc[:, :], -1.0 / M, None, ALU.mult))
                filler("cov")
                dve.wait_ge(e["e1c"], n1)
                assemble("e0c", "tdonec", "sc")
                filler("cov_assemble")
                dve.wait_ge(e["s01c"], n1)
                dve.wait_ge(e["sc"], n1)
                for k in range(KB):
                    last = stt(out=S[:, k, :], in0=MA[:, 0:C], scalar=nsc[:, k:k + 1], in1=S[:, k, :],
                               op0=ALU.mult, op1=ALU.add)
                link(last)
                diag(td, [S[:, k, k * P:(k + 1) * P] for k in range(KB)]).then_inc(e["td"], 1)
                filler("cov_mirror")
                dve.wait_ge(e["trps"], n1)
                link(nc.vector.reduce_sum(tr[:, :], MA[:, 256:258], AX.X))
                link(nc.vector.reciprocal(itr[:, :], tr[:, :]))
                link(ts(Cm[:, :, :], S[:, :, :], itr[:, 0:1], None, ALU.mult))
                ts(tr[:, :], tr[:, :], 1.0 / M, None, ALU.mult).then_inc(e["tr"], 1)
                stt(out=YZ[:, :, 1, :], in0=Cm[:, :, :], scalar=-0.5, in1=i15[:, :, :], op0=ALU.mult,
                    op1=ALU.add).then_inc(e["z0"], 1)
                filler("trace")
                filler("normal")
                for i in range(NS_ITER - 3):
                    dve.wait_ge(zy_done, bns + (i + 1))
                    stt(out=Tm[:, :, :], in0=MB[:, :].rearrange("p (k c) -> p k c", k=KB), scalar=-0.5,
                        in1=i15[:, :, :], op0=ALU.mult, op1=ALU.add).then_inc(t_ready, 1)
                    filler("zy")
                    dve.wait_ge(tyz_done, bns + (i + 1))
                    cp(YZ[:, 1].rearrange("p a c -> p (a c)"), MB[:, :]).then_inc(yz_dve, 1)
                    if i < NS_ITER - 4:
                        filler("tyz")
                dve.wait_ge(yz_act, bns + (NS_ITER - 3))
                dve.wait_ge(yz_dve, bns + (NS_ITER - 3))
                link(nc.vector.reduce_sum(vec[:, 0, :], YZ[:, :, 0, :], AX.X))
                stationary(vec[:, 0, :]).then_inc(pair_in, 1)
                filler("tyz")
                for i in range(PAIRS):
                    dve.wait_ge(pair_ps, bpair + (i + 1))
                    q = vec[:, 2, :] if i == 1 else tmp[:, :]
                    for k in range(KB):
                        last = row_products(q[:, k:k + 1], MA[:, 0:C], YZ[:, k, 1, :], Tm[:, k, :])
                    link(last)
                    if i != 1:
                        link(stt(out=vec[:, i + 1, :], in0=vec[:, i, :], scalar=3.0, in1=tmp[:, :], op0=ALU.mult,
                                 op1=ALU.subtract))
                    if i + 1 < PAIRS:
                        stationary(vec[:, i + 1, :]).then_inc(pair_in, 1)
                        filler("pair")
                link(stt(out=tmp[:, :], in0=vec[:, 1, :], scalar=12.0, in1=vec[:, PAIRS, :], op0=ALU.mult,
                         op1=ALU.subtract))
                dve.wait_ge(e["sq"], n1)
                link(ts(tmp[:, :], tmp[:, :], sq[:, 0:1], 0.0625 / C, ALU.mult, ALU.mult))
                stationary(tmp[:, :]).then_inc(e["y0c"], 1)
                filler("pair")
                dve.wait_ge(e["w1ps"], n1)
                link(tt(Tm[:, 0, :], MA[:, 0:C], b1r[:, :], ALU.add))
                link(ts(Tm[:, 0, :], Tm[:, 0, :], 0.0, None, ALU.max))
                for k in range(KB):
                    last = row_products(tmp[:, k:k + 1], Tm[:, 0, :], w2r[:, k, :], Cm[:, k, :])
                link(last)
                tt(z2[:, :], tmp[:, :], b2c[:, :], ALU.add).then_inc(e["z2"], 1)
                filler("w1")
                dve.wait_ge(e["ez"], n1)
                link(ts(tmp[:, :], ez[:, :], 1.0, None, ALU.add))
                link(nc.vector.reciprocal(y2[:, :], tmp[:, :]))
                link(tt(tmp[:, :], y2[:, :], r1[:, :], ALU.mult))
                ts(ab[:, 0, :], tmp[:, :], 1.0, None, ALU.add)
                link(tt(ez[:, :], tmp[:, :], acol[:, :], ALU.mult))
                link(tt(ab[:, 1, :], ez[:, :], bcol[:, :], ALU.add))
                diagonals(ab[:, :, :].rearrange("p n k -> p (n k)"), 2).then_inc(e["dg2"], 1)
                filler("alpha")
                dve.wait_ge(e["rows2"], n1)
                tt(prod[:, :, :], Wm[:, :, :], MB[:, 0:C].rearrange("p (a c) -> p a c", a=1).broadcast_to([P, KB, C]),
                   ALU.mult).then_inc(e["wfh"], 1)
                dve.wait_ge(even_done, b * (GRAN // 2) + 1)
                dve.wait_ge(odd_done, b * (GRAN // 2) + 1)
                cp(beta[:, :], MB[:, C:2 * C])
                dve.wait_ge(e["wf"], n1)
                tt(wf[:, :, 1, :], prod[:, :, :], wf[:, :, 0, :], ALU.subtract).then_inc(e["ab"], 1)
                filler("gate")
                assert links[0] == DVE_LINKS, links[0]

            cycles(0, 0, CYC_A, 0)
            dve.wait_ge(const_in, 4 * 16)
            dve.wait_ge(w2_ok, 2)
            middle(0, 1, OPENING, a_of=1)
            with dve.Fori(1, B - 1) as b:
                ba = dve.snap(b + 1)
                middle(b, ba, STEADY, c_of=dve.snap(b - 1), a_of=ba)
                cycles(ba, A_CYCLES_BESIDE, CYC_A, L_AHEAD)
            middle(B - 1, B, CLOSING, c_of=B - 2)
            pass_c(B - 1)

        @block.tensor
        def _(pe):
            mm = nc.tensor.matmul
            pe.wait_ge(pool_const, 4)
            pe.sem_inc(hl_free, HL)
            pe.sem_inc(o_done, HT)
            pe.sem_inc(t_done, GCYC)

            def transposed(ps, src):
                for m in range(KB):
                    for k in range(KB):
                        last = nc.tensor.transpose(ps[:, (KB * m + k) * P:(KB * m + k + 1) * P],
                                                   src[:, k, m * P:(m + 1) * P], ident[:, :])
                return last
            def zero(ps, n, first, last):
                return mm(ps[:, 0:n], zero16[:, 0:P], zero16[:, 0:n], start=first, stop=last)

            def open_gram():
                zero(P0, 2 * C, True, False)
                zero(P1, 3 * P, True, False)

            def close_gram():
                zero(P0, 2 * C, False, True)
                zero(P1, 3 * P, False, True).then_inc(e["gram"], 1)

            def gram_group(b32, g):
                pe.wait_ge(l_done, b32 + (g + 1 + AG_PER_CHUNK * XA))
                for t in range(AG):
                    h = hl[:, g % HL, t, :]
                    mm(P0[:, :], h[:, 0:P], h, start=False, stop=False)
                    last = mm(P1[:, 0:3 * P], h[:, P:C], h[:, P:2 * C], start=False, stop=False)
                last.then_inc(hl_free, 1)

            def cycles(b, lo, hi):
                with pe.Fori(lo, hi) as i:
                    b32 = pe.snap(b * (CYC_A * GPC) + i * GPC)
                    for q in range(GPC):
                        gram_group(b32, q)

            def transposes(g0, c16, g):
                c, i = divmod(g, CG)
                if i == 0:
                    pe.wait_ge(xc_in[c % XC], c16 + 16 * (c // XC + 1))
                pe.wait_ge(lT_done, g0 + (g + 1))
                for k in range(KB):
                    for t in range(2):
                        src = xc[:, c % XC, (2 * i + t) * C + k * P:(2 * i + t) * C + (k + 1) * P]
                        last = nc.tensor.transpose(TP[g % TB][:, (2 * k + t) * P:(2 * k + t + 1) * P], src, ident[:, :])
                last.then_inc(t_done, 1)

            def products(g0, h0, g):
                pe.wait_ge(lT_done, g0 + (g + 1 + TB))
                pe.wait_ge(copied if g % 2 else even_done, h0 + (g // 2 + 1))
                for t in range(2):
                    o = OP[g % TB][:, t * C:(t + 1) * C]
                    terms = [(a, k, w) for k in range(KB) for a, w in ((hT, 0), (hT, 1), (lT, 0))]
                    for n, (a, k, w) in enumerate(terms):
                        last = mm(o, a[:, g % HT, k, t, :], wf[:, k, w, :], start=(n == 0), stop=(n + 1 == len(terms)))
                last.then_inc(o_done, 1)

            def c_ready(n1):
                pe.wait_ge(e["ab"], n1)

            def pass_c(b):
                for g in range(AHEAD):
                    transposes(b * GRAN, b * (CHUNKS // XC * 16), g)
                c_ready(b + 1)
                cycles = GRAN // GCYC
                with pe.Fori(0, cycles - 1) as i:
                    g0 = pe.snap(b * GRAN + i * GCYC)
                    h0 = pe.snap(b * (GRAN // 2) + i * (GCYC // 2))
                    c16 = pe.snap(b * (CHUNKS // XC * 16) + i * 16)
                    for g in range(GCYC):
                        transposes(g0, c16, g + AHEAD)
                        products(g0, h0, g)
                h0 = b * (GRAN // 2) + (cycles - 1) * (GCYC // 2)
                g0 = b * GRAN + (cycles - 1) * GCYC
                c16 = b * (CHUNKS // XC * 16) + (cycles - 1) * 16
                for g in range(GCYC):
                    if g + AHEAD < GCYC:
                        transposes(g0, c16, g + AHEAD)
                    products(g0, h0, g)

            def mat(dst, lhs, rhs, w=C):
                for m in range(KB):
                    for k in range(KB):
                        last = mm(dst(m), lhs(k)[:, m * P:(m + 1) * P], rhs(k), start=(k == 0), stop=(k == KB - 1))
                return last

            def mirror(e0n, e1n, tn, sn, mn, n1, filler, stage, between):
                tr = nc.tensor.transpose
                pe.wait_ge(e[e0n], n1)
                pe.wait_ge(e[e1n], n1)
                tr(MB[:, 0:P], e0[:, C:C + P], ident[:, :])
                tr(MB[:, P:2 * P], e1[:, P:2 * P], ident[:, :])
                tr(MB[:, 2 * P:3 * P], e1[:, 2 * P:3 * P], ident[:, :]).then_inc(e[tn], 1)
                between()
                filler(stage)
                pe.wait_ge(e[sn], n1)
                tr(MB[:, 3 * P:4 * P], S[:, 0, P:C], ident[:, :]).then_inc(e[mn], 1)

            def middle(b, n1, plan, c_of=None, a_of=None):
                if a_of is not None:
                    b32 = pe.snap(a_of * (CYC_A * GPC))
                if c_of is not None:
                    c_ready(b)
                    g0 = pe.snap(c_of * GRAN)
                    h0 = pe.snap(c_of * (GRAN // 2))
                    c16 = pe.snap(c_of * (CHUNKS // XC * 16))
                    for g in range(AHEAD):
                        transposes(g0, c16, g)

                def c_step(g):
                    if g + AHEAD < GRAN:
                        transposes(g0, c16, g + AHEAD)
                    products(g0, h0, g)

                def a_step(g):
                    if g == 0:
                        pe.wait_ge(e["e0"], n1)
                        pe.wait_ge(e["e1"], n1)
                        open_gram()
                    gram_group(b32, g)

                filler = filling(plan, c_step, a_step)
                b16 = pe.snap(b * 2 * UNITS)
                bcm = pe.snap(b * len(CROPMM))
                bns = pe.snap(b * (NS_ITER - 3))
                bpair = pe.snap(b * PAIRS)
                filler("gram")
                filler("sums")

                def channel_sums():
                    pe.wait_ge(e["acc"], n1)
                    mm(MA[:, 0:C], onesf[:, :], accd[:, 0:C], start=True, stop=True).then_inc(e["sbc"], 1)
                mirror("e0", "e1", "tdone", "st", "mirror", n1, filler, "assemble", channel_sums)
                filler("mirror")
                pe.wait_ge(e["gst"], n1)
                pe.wait_ge(e["s01"], n1)
                pe.wait_ge(crop_in, n1 * 32)
                for u in range(UNITS):
                    for k in range(KB):
                        if c_of is not None:
                            pe.wait_ge(crop_l, b16 + (2 * u + k + 1))
                        elif u >= 2:
                            pe.wait_ge(crop_l, b16 + (2 * u + k - 1))
                        for t in range(UPX // CW):
                            last = nc.tensor.transpose(crop_bank(u, k, c_of)[:, t * CW:(t + 1) * CW],
                                                       xcr[:, u * (UPX // CW) + t, k * P:(k + 1) * P], ident[0:CW, 0:CW])
                        last.then_inc(crop_t, 1)
                    filler("crop")
                pe.wait_ge(crop_l, b16 + (2 * UNITS + 2))
                pe.sem_inc(e["crop_free"], 1)
                pe.wait_ge(e["gst"], n1)
                mm(MA[:, C:C + 4], grp[:, :], st1[:, :], start=True, stop=True).then_inc(e["means"], 1)
                filler("means")
                filler("stats")
                pe.wait_ge(e["dg"], n1)
                mm(MB[:, :], onesf[:, :], dg[:, 0:2].rearrange("p n k c -> p (n k c)"), start=True, stop=True)
                mm(MA[:, 0:C], onesf[:, :], dg[:, 2].rearrange("p k c -> p (k c)"), start=True,
                   stop=True).then_inc(e["rows"], 1)
                for stage in NAMES[NAMES.index("rows"):NAMES.index("weights")]:
                    filler(stage)
                pe.wait_ge(e["wdone"], n1)
                transposed(cov_banks(a_of, c_of)[1], Wm).then_inc(e["wT_ps"], 1)
                mat(lambda m: (MA, MB)[m][:, 0:C + 2], lambda k: Wm[:, k, :], lambda k: Sx[:, k, :]).then_inc(e["proj"], 1)
                filler("weights")
                pe.wait_ge(e["st1"], n1)
                mm(MA[:, C:C + 4], grp[:, :], st1[:, :], start=True, stop=True).then_inc(e["gst1"], 1)
                filler("squares")
                filler("stats1")
                pe.wait_ge(e["wsp"], n1)
                pe.wait_ge(e["ve1"], n1)
                for i, (jj, m) in enumerate(CROPMM):
                    c0, n = 2 * jj * C, min(2, NJ - 2 * jj) * C
                    pe.wait_ge(gh_done, bcm + (i + 1))
                    terms = [(w, k, a) for k in range(KB) for w, a in ((0, 0), (1, 0), (0, 1))]
                    for j, (w, k, a) in enumerate(terms):
                        last = mm((MA, MB)[m][:, 0:n], wsp[:, k, w, m * P:(m + 1) * P], xcT[:, k, a, c0:c0 + n],
                                  start=(j == 0), stop=(j + 1 == len(terms)))
                    last.then_inc(cm_done, 1)
                    filler("crop_product")
                pe.wait_ge(ghl_done, bcm + (len(CROPMM) + 2))
                pe.wait_ge(gh_done, bcm + (len(CROPMM) + 2))
                q0, q1 = cov_banks(a_of, c_of)
                pe.wait_ge(e["wT"], n1)
                for i in range(NJ * KB):
                    j, k = divmod(i, KB)
                    g = ghl[:, k, j, :, :].rearrange("p a c -> p (a c)")
                    io = dict(start=(i == 0), stop=(i + 1 == NJ * KB))
                    mm(q0[:, :], g[:, 0:P], g, **io)
                    mm(q1[:, 0:3 * P], g[:, P:C], g[:, P:2 * C], **io)
                pe.wait_ge(gs_done, n1 * (2 * (NJ - 1)))
                for k in range(KB):
                    last = mm(MA[:, 0:C], onesf[:, :], gsum[:, k, :], start=(k == 0), stop=(k == KB - 1))
                last.then_inc(e["cov"], 1)
                filler("cov")
                mirror("e0c", "e1c", "tdonec", "sc", "mirrorc", n1, filler, "cov_assemble", lambda: None)
                filler("cov_mirror")
                pe.wait_ge(e["td"], n1)
                mm(MA[:, C:C + 2], onesf[:, :], td[:, :], start=True, stop=True).then_inc(e["trps"], 1)
                filler("trace")
                pe.wait_ge(e["z0"], n1)
                mat(lambda m: MA[:, m * C:(m + 1) * C], lambda k: Cm[:, k, :], lambda k: YZ[:, k, 1, :]).then_inc(e["y0ps"], 1)
                filler("normal")
                pe.wait_ge(e["y0"], n1)
                pe.wait_ge(e["s01c"], n1)
                for i in range(NS_ITER - 3):
                    if i:
                        pe.wait_ge(yz_act, bns + i)
                        pe.wait_ge(yz_dve, bns + i)
                    mat(lambda m: MB[:, m * C:(m + 1) * C], lambda k: YZ[:, k, 1, :],
                        lambda k: YZ[:, k, 0, :]).then_inc(zy_done, 1)
                    filler("zy")
                    pe.wait_ge(t_ready, bns + (i + 1))
                    mat(lambda m: (MA, MB)[m][:, :], lambda k: Tm[:, k, :],
                        lambda k: YZ[:, k].rearrange("p a c -> p (a c)")).then_inc(tyz_done, 1)
                    filler("tyz")
                def times(matrix):
                    for k in range(KB):
                        last = mm(MA[:, 0:C], dg[:, 2, k, :], matrix(k), start=(k == 0), stop=(k == KB - 1))
                    return last

                for i in range(PAIRS):
                    pe.wait_ge(pair_in, bpair + (i + 1))
                    times(lambda k: YZ[:, k, 0, :]).then_inc(pair_ps, 1)
                    filler("pair")
                pe.wait_ge(e["y0c"], n1)
                times(lambda k: w1c[:, k, :]).then_inc(e["w1ps"], 1)
                filler("w1")
                filler("alpha")
                pe.wait_ge(e["dg2"], n1)
                mm(MB[:, :], onesf[:, :], dg[:, 0:2].rearrange("p n k c -> p (n k c)"), start=True,
                   stop=True).then_inc(e["rows2"], 1)
                filler("gate")

            open_gram()
            cycles(0, 0, 1)
            pe.wait_ge(gam_in, 16)
            pe.wait_ge(const_in, 4 * 16)
            mm(MA[:, 0:1], onesf[0:1, :], gam0[0:1, 0:1], start=True, stop=True)
            transposed(MB, prod).then_inc(w2_ps, 1)
            cycles(0, 1, CYC_A)
            close_gram()
            pe.wait_ge(w2_ok, 2)
            middle(0, 1, OPENING, a_of=1)
            close_gram()
            with pe.Fori(1, B - 1) as b:
                ba = pe.snap(b + 1)
                middle(b, ba, STEADY, c_of=pe.snap(b - 1), a_of=ba)
                cycles(ba, A_CYCLES_BESIDE, CYC_A)
                close_gram()
            middle(B - 1, B, CLOSING, c_of=B - 2)
            pass_c(B - 1)


_INS = ["x", "L0_conv_gamma", "L1_conv_w1", "L1_conv_b1", "L1_conv_w2", "L1_conv_b2"]


def kernel(**inputs):
    import numpy as _np
    import concourse.bacc as _bacc
    from concourse import mybir as _mybir
    from concourse.bass_utils import run_bass_kernel_spmd as _run

    nc = _bacc.Bacc("TRN2", target_bir_lowering=False, num_devices=1)
    arrays, args = {}, []
    for name in _INS:
        a = _np.ascontiguousarray(inputs[name])
        if a.ndim == 0:
            a = a.reshape(1)
        arrays[f"in_{name}"] = a
        args.append(nc.dram_tensor(f"in_{name}", a.shape, _mybir.dt.from_np(a.dtype), kind="ExternalInput").ap())
    args.append(nc.dram_tensor("out_0", (B, H, W_, C), f32, kind="ExternalOutput").ap())
    build(nc, *args)
    r = _run(nc, [arrays], core_ids=[0])
    return r.results[0]["out_0"]
```
